# Optimizing a Trainium2 kernel written in Bass

```python
import numpy as np
import jax
import jax.numpy as jnp

def _softmax(x, axis=-1):
    return jax.nn.softmax(x, axis=axis)

def _gelu(x):
    return jax.nn.gelu(x, approximate=True)

def _silu(x):
    return jax.nn.silu(x)

def _sigmoid(x):
    return jax.nn.sigmoid(x)

def _layernorm(x, axis=-1, eps=1e-05):
    m = jnp.mean(x, axis=axis, keepdims=True)
    v = jnp.var(x, axis=axis, keepdims=True)
    return (x - m) / jnp.sqrt(v + eps)

def _scatter_add(tgt, idx, src, axis=0):
    return tgt.at[idx].add(src)

def _segment_sum(src, seg, n):
    return jax.ops.segment_sum(src, seg, n)
kernel_name = 'mk_seq_preln_d1_jaxref_r8_8f780b'

def setup_inputs(seed: int=0):
    np.random.seed(seed)
    _w = jnp.asarray

    def _L0_attn_setup():
        import jax, jax.numpy as jnp
        import numpy as np
        import math
        D_MODEL = 128
        NUM_HEADS = 16
        HEAD = D_MODEL // NUM_HEADS
        EPS = 1e-05

        def _layernorm(x, w, b):
            mean = jnp.mean(x, axis=-1, keepdims=True)
            var = jnp.var(x, axis=-1, keepdims=True)
            return (x - mean) * w / jnp.sqrt(var + EPS) + b
        key = jax.random.key(seed)
        ks = jax.random.split(key, 5)
        x = jax.random.normal(ks[0], (2, 256, D_MODEL), dtype=jnp.float32)
        wq = jax.random.uniform(ks[1], (NUM_HEADS, D_MODEL, HEAD), dtype=jnp.float32) * 0.02
        wk = jax.random.uniform(ks[2], (NUM_HEADS, D_MODEL, HEAD), dtype=jnp.float32) * 0.02
        wv = jax.random.uniform(ks[3], (NUM_HEADS, D_MODEL, HEAD), dtype=jnp.float32) * 0.02
        wo = jax.random.uniform(ks[4], (D_MODEL, D_MODEL), dtype=jnp.float32) * 0.02
        ln_w = jnp.ones((D_MODEL,), dtype=jnp.float32)
        ln_b = jnp.zeros((D_MODEL,), dtype=jnp.float32)
        return {'x': x, 'ln_w': ln_w, 'ln_b': ln_b, 'wq': wq, 'wk': wk, 'wv': wv, 'wo': wo}
    _L0_attn_in = _L0_attn_setup()

    def _L0_ffn_setup():
        import jax, jax.numpy as jnp
        import numpy as np
        B, T, H, F, E, TOPK = (4, 128, 128, 512, 8, 2)

        def _moe_forward(x, rw, rb, w1, b1, w2, b2, sw1, sb1, sw2, sb2):
            Bb, Tt, Hh = x.shape
            N = Bb * Tt
            Ee = rw.shape[0]
            cap = max(1, int(N / Ee * 1.0))
            xf = x.reshape(N, Hh)
            logits = xf @ rw.T + rb
            g_soft = jax.nn.softmax(logits, axis=-1)
            _, idx = jax.lax.top_k(g_soft, TOPK)
            primary, second = (idx[:, 0], idx[:, 1])
            ohp = jax.nn.one_hot(primary, Ee, dtype=jnp.int32)
            posp = jnp.cumsum(ohp, axis=0) - ohp
            pos_tok = jnp.take_along_axis(posp, primary[:, None], 1)[:, 0]
            keep_primary = pos_tok < cap
            used = jnp.minimum(ohp.sum(axis=0), cap)
            overflow = ~keep_primary
            ohs = jax.nn.one_hot(second, Ee, dtype=jnp.int32) * overflow[:, None].astype(jnp.int32)
            poss = jnp.cumsum(ohs, axis=0) - ohs
            pos2 = jnp.take_along_axis(poss, second[:, None], 1)[:, 0]
            take2 = overflow & (used[second] + pos2 < cap)
            assign = jnp.where(keep_primary, primary, jnp.where(take2, second, -1))
            overflow = overflow & ~take2
            h = jax.nn.gelu(jnp.einsum('nh,ehf->enf', xf, w1) + b1[:, None, :], approximate=False)
            stack = jnp.einsum('enf,efh->enh', h, w2) + b2[:, None, :]
            one_hot_a = jax.nn.one_hot(assign, Ee, dtype=stack.dtype)
            y = jnp.einsum('enh,ne->nh', stack, one_hot_a)
            y_fb = jax.nn.gelu(xf @ sw1 + sb1, approximate=False) @ sw2 + sb2
            y = jnp.where(overflow[:, None], y_fb, y)
            return y.reshape(Bb, Tt, Hh)
        key = jax.random.key(seed)
        ks = jax.random.split(key, 12)
        s = 0.02
        return {'x': jax.random.normal(ks[0], (B, T, H), dtype=jnp.float32), 'rw': jax.random.normal(ks[1], (E, H), dtype=jnp.float32) * s, 'rb': jnp.zeros((E,), dtype=jnp.float32), 'w1': jax.random.normal(ks[2], (E, H, F), dtype=jnp.float32) * s, 'b1': jnp.zeros((E, F), dtype=jnp.float32), 'w2': jax.random.normal(ks[3], (E, F, H), dtype=jnp.float32) * s, 'b2': jnp.zeros((E, H), dtype=jnp.float32), 'sw1': jax.random.normal(ks[4], (H, F), dtype=jnp.float32) * s, 'sb1': jnp.zeros((F,), dtype=jnp.float32), 'sw2': jax.random.normal(ks[5], (F, H), dtype=jnp.float32) * s, 'sb2': jnp.zeros((H,), dtype=jnp.float32)}
    _L0_ffn_in = _L0_ffn_setup()
    _d = {'L0_attn_x': _L0_attn_in['x'], 'L0_attn_ln_w': _L0_attn_in['ln_w'], 'L0_attn_ln_b': _L0_attn_in['ln_b'], 'L0_attn_wq': _L0_attn_in['wq'], 'L0_attn_wk': _L0_attn_in['wk'], 'L0_attn_wv': _L0_attn_in['wv'], 'L0_attn_wo': _L0_attn_in['wo'], 'L0_ffn_rw': _L0_ffn_in['rw'], 'L0_ffn_rb': _L0_ffn_in['rb'], 'L0_ffn_w1': _L0_ffn_in['w1'], 'L0_ffn_b1': _L0_ffn_in['b1'], 'L0_ffn_w2': _L0_ffn_in['w2'], 'L0_ffn_b2': _L0_ffn_in['b2'], 'L0_ffn_sw1': _L0_ffn_in['sw1'], 'L0_ffn_sb1': _L0_ffn_in['sb1'], 'L0_ffn_sw2': _L0_ffn_in['sw2'], 'L0_ffn_sb2': _L0_ffn_in['sb2']}
    _x0 = _d['L0_attn_x']
    _d['L0_attn_x'] = jax.random.normal(jax.random.fold_in(jax.random.key(seed), 1), (4, 1024, 128), dtype=_x0.dtype)
    del _x0
    return _d

def reference(L0_attn_x, L0_attn_ln_w, L0_attn_ln_b, L0_attn_wq, L0_attn_wk, L0_attn_wv, L0_attn_wo, L0_ffn_rw, L0_ffn_rb, L0_ffn_w1, L0_ffn_b1, L0_ffn_w2, L0_ffn_b2, L0_ffn_sw1, L0_ffn_sb1, L0_ffn_sw2, L0_ffn_sb2):

    def _L0_attn_ref(x, ln_w, ln_b, wq, wk, wv, wo):
        import jax, jax.numpy as jnp
        import numpy as np
        import math
        D_MODEL = 128
        NUM_HEADS = 16
        HEAD = D_MODEL // NUM_HEADS
        EPS = 1e-05

        def _layernorm(x, w, b):
            mean = jnp.mean(x, axis=-1, keepdims=True)
            var = jnp.var(x, axis=-1, keepdims=True)
            return (x - mean) * w / jnp.sqrt(var + EPS) + b
        y = _layernorm(x, ln_w, ln_b)
        seq_len = y.shape[-2]
        q = jnp.einsum('bsd,hde->bhse', y, wq)
        k = jnp.einsum('bsd,hde->bhse', y, wk)
        v = jnp.einsum('bsd,hde->bhse', y, wv)
        scores = jnp.einsum('bhse,bhte->bhst', q, k) / math.sqrt(HEAD)
        causal = jnp.triu(jnp.full((seq_len, seq_len), -jnp.inf, dtype=scores.dtype), k=1)
        scores = scores + causal
        weights = jax.nn.softmax(scores, axis=-1)
        attn = jnp.einsum('bhst,bhte->bshe', weights, v)
        attn = attn.reshape(*attn.shape[:-2], -1)
        out = attn @ wo
        return out + x

    def _L0_ffn_ref(x, rw, rb, w1, b1, w2, b2, sw1, sb1, sw2, sb2):
        import jax, jax.numpy as jnp
        import numpy as np
        B, T, H, F, E, TOPK = (4, 128, 128, 512, 8, 2)

        def _moe_forward(x, rw, rb, w1, b1, w2, b2, sw1, sb1, sw2, sb2):
            Bb, Tt, Hh = x.shape
            N = Bb * Tt
            Ee = rw.shape[0]
            cap = max(1, int(N / Ee * 1.0))
            xf = x.reshape(N, Hh)
            logits = xf @ rw.T + rb
            g_soft = jax.nn.softmax(logits, axis=-1)
            _, idx = jax.lax.top_k(g_soft, TOPK)
            primary, second = (idx[:, 0], idx[:, 1])
            ohp = jax.nn.one_hot(primary, Ee, dtype=jnp.int32)
            posp = jnp.cumsum(ohp, axis=0) - ohp
            pos_tok = jnp.take_along_axis(posp, primary[:, None], 1)[:, 0]
            keep_primary = pos_tok < cap
            used = jnp.minimum(ohp.sum(axis=0), cap)
            overflow = ~keep_primary
            ohs = jax.nn.one_hot(second, Ee, dtype=jnp.int32) * overflow[:, None].astype(jnp.int32)
            poss = jnp.cumsum(ohs, axis=0) - ohs
            pos2 = jnp.take_along_axis(poss, second[:, None], 1)[:, 0]
            take2 = overflow & (used[second] + pos2 < cap)
            assign = jnp.where(keep_primary, primary, jnp.where(take2, second, -1))
            overflow = overflow & ~take2
            h = jax.nn.gelu(jnp.einsum('nh,ehf->enf', xf, w1) + b1[:, None, :], approximate=False)
            stack = jnp.einsum('enf,efh->enh', h, w2) + b2[:, None, :]
            one_hot_a = jax.nn.one_hot(assign, Ee, dtype=stack.dtype)
            y = jnp.einsum('enh,ne->nh', stack, one_hot_a)
            y_fb = jax.nn.gelu(xf @ sw1 + sb1, approximate=False) @ sw2 + sb2
            y = jnp.where(overflow[:, None], y_fb, y)
            return y.reshape(Bb, Tt, Hh)
        return _moe_forward(x, rw, rb, w1, b1, w2, b2, sw1, sb1, sw2, sb2)
    x = L0_attn_x
    x = x + _L0_attn_ref(_layernorm(x, axis=-1), L0_attn_ln_w, L0_attn_ln_b, L0_attn_wq, L0_attn_wk, L0_attn_wv, L0_attn_wo)
    x = x + _L0_ffn_ref(_layernorm(x, axis=-1), L0_ffn_rw, L0_ffn_rb, L0_ffn_w1, L0_ffn_b1, L0_ffn_w2, L0_ffn_b2, L0_ffn_sw1, L0_ffn_sb1, L0_ffn_sw2, L0_ffn_sb2)
    return x

_drawn_inputs = setup_inputs


def setup_inputs(seed=0):
    import zlib

    import numpy as np

    out = dict(_drawn_inputs(seed))
    spreads = {'L0_attn_ln_w': (1.0, 0.6),
     'L0_attn_ln_b': (0.0, 0.8),
     'L0_ffn_rb': (0.0, 0.1),
     'L0_ffn_b1': (0.0, 2.0),
     'L0_ffn_b2': (0.0, 0.8),
     'L0_ffn_sb1': (0.0, 0.8),
     'L0_ffn_sb2': (0.0, 1.871)}
    factors = {'L0_attn_wq': 8.0,
     'L0_attn_wk': 8.0,
     'L0_attn_wv': 8.0,
     'L0_attn_wo': 8.0,
     'L0_ffn_sw1': 5.48,
     'L0_ffn_sw2': 4.926,
     'L0_ffn_w1': 8.0,
     'L0_ffn_w2': 2.73}
    for name, (base, spread) in spreads.items():
        noise = np.random.default_rng([zlib.crc32(name.encode()), seed]).standard_normal(out[name].shape)
        drawn = base * np.exp(spread * noise) if base else spread * noise
        out[name] = jnp.asarray(drawn.astype(out[name].dtype))
    for name, factor in factors.items():
        out[name] = (out[name] * factor).astype(out[name].dtype)
    return out
```

```python
from contextlib import ExitStack

import concourse.bass as bass
from concourse import mybir

ALU = mybir.AluOpType
ACT = mybir.ActivationFunctionType
AX = mybir.AxisListType
F32 = mybir.dt.float32
BF16 = mybir.dt.bfloat16
U32 = mybir.dt.uint32

P = 128
PARTS = 3
TERMS = PARTS * PARTS
MASKED = -3.0e38
EPS = 1e-5
TURN_LAG = 8
ROWS = 3
COLS = 3


def attention_plan(S, HG):
    tiles = S // P
    half = 512
    rounds = []
    for qh in range(S // half):
        for kt in range((qh + 1) * half // P):
            q0 = max(qh * half, kt * P)
            rounds.append((qh, kt, q0, (qh + 1) * half - q0))
    last = [(qt, qt * P // half) for qt in range(tiles)]
    whole = [(qt, c) for qt in reversed(range(tiles)) for c in range(qt * P // half)]
    last.sort(key=lambda x: x[0] * P % half)
    order, wide = [], whole + last[len(last) - (len(last) - len(whole)) // 2:]
    narrow = last[:len(last) - (len(last) - len(whole)) // 2]
    while wide or narrow:
        order += wide[:1] + narrow[:1]
        wide, narrow = wide[1:], narrow[1:]
    per = len(order)
    leads = [(1, HG - 1, *x) for x in order]
    for h in range(HG - 1):
        leads += [(2, h, *x) for x in order]
    leads.insert(per + TURN_LAG, None)
    return rounds, order, leads


def width(qt, c):
    return min((qt + 1) * P - c * 512, 512)


def spread(rounds, leads, AHEAD, HG):
    n_rounds = len(rounds)
    cost = []
    for k in range(n_rounds):
        nxt = rounds[(k + AHEAD) % n_rounds][3]
        for h in range(HG):
            cost.append(nxt + (rounds[k][3] * 4 if h == 0 else 0))
    total = sum(cost)
    need = [0 if x is None else width(x[2], x[3]) for x in leads]
    whole = sum(need)
    out, at, done, spent = [], 0, 0, 0
    for c in cost:
        spent += c
        here = []
        while at < len(leads) and (done + need[at] / 2) * total <= spent * whole:
            here.append(at)
            done += need[at]
            at += 1
        out.append(here)
    out[-1] += list(range(at, len(leads)))
    return out


def build(nc, x, ln_w, ln_b, wq, wk, wv, wo, rw, rb, w1, b1, w2, b2, sw1, sb1, sw2, sb2, out, debug=None):
    B, S, D = x.shape
    H, _, HD = wq.shape
    HG = 4
    G = H // HG
    T = S // P
    NT = B * T
    N = B * S
    E, _, F = w1.shape
    FC = F // P
    CAP = max(1, N // E)
    VW = HD + 1
    VWIN = (HG - 1) * VW + 32
    VALL = (H - HG) * VW + VWIN
    STACK = TERMS * HD
    CH = 4
    NCH = NT // CH
    QSCALE = float(HD) ** -0.5
    assert D == P and H * HD == P and S % 512 == 0

    rounds, order, leads = attention_plan(S, HG)
    NR = len(rounds)
    AHEAD = 2
    after = spread(rounds, leads, AHEAD, HG)
    NL = len(leads)
    NU = NL - 1
    PER = len(order)
    PRO = [(0, h, *x) for h in range(HG) for x in order] + \
          [(1, h, *x) for h in range(HG - 1) for x in order]
    PRO.insert(HG * PER + TURN_LAG, None)
    assert (len(PRO) - 1) % ROWS == 0 and (G * NL - 1) % ROWS == 0
    diag = [r for r, (qh, kt, q0, n) in enumerate(rounds) if kt * P == q0]

    qd = nc.dram_tensor("q_parts", [B, PARTS, P, S], BF16).ap()
    kd = nc.dram_tensor("k_parts", [B, PARTS, P, S], BF16).ap()
    vd = nc.dram_tensor("v_windows", [B, G, P, T, VWIN], F32).ap()

    with ExitStack() as ctx:
        def sb(name, shape, dt=F32):
            return ctx.enter_context(nc.sbuf_tensor(name, shape, dt))

        def sem(name):
            return ctx.enter_context(nc.semaphore(name))

        psum = ctx.enter_context(nc.psum_tensor("psum", [P, 8, 512], F32))

        ident = sb("ident", [P, P])
        identb = sb("identb", [P, P], BF16)
        tokens = sb("tokens", [P, B, T, D])
        attn = sb("attn", [P, B, T, D])

        s_const = sem("s_const")

        with nc.Block() as block:
            @block.gpsimd
            def _(pool):
                pool.memset(ident[:], 0.0).then_inc(s_const, 1)
                pool.wait_ge(s_const, 1)
                pool.affine_select(out=ident[:], in_=ident[:], compare_op=ALU.not_equal, fill=1.0, base=0,
                                   pattern=[[-1, P]], channel_multiplier=1).then_inc(s_const, 1)
                pool.wait_ge(s_const, 2)
                pool.tensor_copy(identb[:], ident[:]).then_inc(s_const, 1)

        L0 = dict(locals())
        prepare(nc, ctx, sem, locals())
        attention(nc, ctx, sem, locals())
        with ExitStack() as late:
            def sb(name, shape, dt=F32):
                return late.enter_context(nc.sbuf_tensor(name, shape, dt))

            ROW = 2 * D + 1
            rowbuf = sb("rowbuf", [P, B, T, ROW])
            xnT = sb("xnT", [D, B, S])
            logits = sb("logits", [P, E, B, T])
            slot = sb("slot", [P, NT], U32)
            sorted_rows = nc.dram_tensor("sorted_rows", [E * CAP + N, ROW], F32).ap()
            project(nc, late, sem, locals() | dict(L0))
            route(nc, late, sem, locals() | dict(L0))
            experts(nc, late, sem, locals() | dict(L0))
        if debug is not None:
            s_dbg = sem("s_dbg")
            with nc.Block() as block:
                @block.sync
                def _(sp):
                    sp.dma_start(debug.rearrange("(b t p) d -> p (b t) d", b=B, p=P), attn[:].rearrange("p b t d -> p (b t) d")).then_inc(s_dbg, 16)
                    sp.wait_ge(s_dbg, 16)


def wait_apart(eng, sem, value, passed):
    eng.wait_ge(sem, value)
    eng.sem_inc(passed, 1)


def prepare(nc, octx, sem, L):
    (x, ln_w, ln_b, wq, wk, wv, tokens, ident, psum, qd, kd, vd) = (
        L[n] for n in "x ln_w ln_b wq wk wv tokens ident psum qd kd vd".split())
    B, S, D, H, HD, HG, G, T, NT, CH, NCH, VW, VWIN, VALL, QSCALE = (
        L[n] for n in "B S D H HD HG G T NT CH NCH VW VWIN VALL QSCALE".split())
    W = CH * P
    with ExitStack() as ctx:
        def sb(name, shape, dt=F32):
            return ctx.enter_context(nc.sbuf_tensor(name, shape, dt))

        wq_s, wk_s, wv_s = sb("wq_s", [D, P]), sb("wk_s", [D, P]), sb("wv_s", [D, P])
        wq_r, wk_r = sb("wq_r", [D, H, HD]), sb("wk_r", [D, H, HD])
        gain, shift = sb("gain", [D, 1]), sb("shift", [D, 1])
        eps = sb("eps", [P, 1])
        stat = sb("stat", [P, 2, 2, CH, 6])
        mv = sb("mv", [P, 2, 2, CH, 2])
        rstd = sb("rstd", [P, 2, 2, CH])
        tmp = sb("tmp", [P, 2, 2, 4, CH])
        z = sb("z", [P, 2, CH, D])
        y = sb("y", [P, 2, CH, D])
        yT = sb("yT", [D, 2, W])
        full = sb("full", [P, 2, 2, W])
        rest = sb("rest", [P, 2, 2, W])
        parts = sb("parts", [P, 2, 2, PARTS, W], BF16)
        vwin = sb("vwin", [P, 2, CH, VALL])

        s_x = [sem(f"s_x{b}") for b in range(B)]
        s_w = sem("s_w")
        s_passed = sem("s_passed_prepare")
        s_wp = sem("s_wp")
        s_vinit = sem("s_vinit")
        s_dve = sem("s_dve")
        s_var = sem("s_var")
        s_sqrt = sem("s_sqrt")
        s_y = sem("s_y")
        s_yt = sem("s_yt")
        s_yT = sem("s_yT")
        s_q, s_k, s_v = sem("s_q"), sem("s_k"), sem("s_v")
        s_p1 = sem("s_p1")
        s_split = sem("s_split")
        s_vw = sem("s_vw")
        s_st = [sem("s_store0"), sem("s_store1")]

        with nc.Block() as block:
            @block.sync
            def _(sp):
                for b in range(B):
                    sp.dma_start(tokens[:, b], x[b].rearrange("(t p) d -> p t d", p=P)).then_inc(s_x[b], 16)
                    if b == 0:
                        for h0, ws in ((0, wq_r), (0, wk_r)):
                            pass
                        sp.dma_start(wq_r[:], wq.rearrange("h d e -> d h e")).then_inc(s_w, 16)
                        sp.dma_start(wk_r[:], wk.rearrange("h d e -> d h e")).then_inc(s_w, 16)
                        sp.dma_start(wv_s[:].rearrange("d (h e) -> d h e", h=H), wv.rearrange("h d e -> d h e")).then_inc(s_w, 16)
                        sp.dma_start(gain[:], ln_w.rearrange("(d o) -> d o", o=1)).then_inc(s_w, 16)
                        sp.dma_start(shift[:], ln_b.rearrange("(d o) -> d o", o=1)).then_inc(s_w, 16)
                with sp.Fori(0, B) as b:
                    for u in range(2):
                        sp.wait_ge(s_split, 4 * b + 2 * u + 2)
                        for a, dst in ((0, qd), (1, kd)):
                            sp.dma_start(dst[b, :, :, u * W:(u + 1) * W].rearrange("i p t -> p i t"),
                                         parts[:, u, a]).then_inc(s_st[u], 16)
                        sp.wait_ge(s_vw, 2 * b + u + 1)
                        for g in range(G):
                            sp.dma_start(vd[b, g, :, u * CH:(u + 1) * CH, :],
                                         vwin[:, u, :, g * HG * VW:g * HG * VW + VWIN]).then_inc(s_st[u], 16)
                for u in range(2):
                    sp.wait_ge(s_st[u], 16 * (2 + G) * B)

            @block.gpsimd
            def _(pool):
                pool.memset(vwin[:, :, :, H * VW:], 0.0).then_inc(s_vinit, 1)
                for u in range(2):
                    pool.memset(vwin[:, u, :, 0:H * VW].rearrange("p t (h v) -> p t h v", v=VW)[:, :, :, HD:], 1.0).then_inc(s_vinit, 1)
                pool.memset(eps[:], EPS).then_inc(s_vinit, 1)

            @block.vector
            def _(dve):
                chain = [0]

                def own(ins):
                    ins.then_inc(s_dve, 1)

                dve.wait_ge(s_w, 80)
                for a, (src, dst) in enumerate(((wq_r, wq_s), (wk_r, wk_s))):
                    dve.tensor_copy(dst[:].rearrange("d (g e h) -> d g e h", g=G, e=HD),
                                    src[:].rearrange("d (g h) e -> d g e h", g=G)).then_inc(s_wp, 1)
                for b in range(B):
                    dve.wait_ge(s_x[b], 16)
                with dve.Fori(0, B) as b:
                    count = 0
                    per = 2 * 9 + 2
                    for u in range(2):
                        for n in range(2):
                            src = tokens[:, b, u * CH:(u + 1) * CH] if n == 0 else z[:, u]
                            dst = z[:, u] if n == 0 else y[:, u]
                            for t in range(CH):
                                last = dve.bn_stats(stat[:, u, n, t], src[:, t])
                            last.then_inc(s_dve, 1)
                            count += 1
                            wait_apart(dve, s_dve, b * 2 * per + count, s_passed)
                            for t in range(CH):
                                last = dve.bn_aggr(mv[:, u, n, t], stat[:, u, n, t:t + 1])
                            last.then_inc(s_dve, 1)
                            count += 1
                            dve.wait_ge(s_dve, b * 2 * per + count)
                            c = tmp[:, u, n]
                            dve.tensor_scalar(c[:, 0], mv[:, u, n, :, 1], EPS, None, ALU.add).then_inc(s_var, 1)
                            dve.wait_ge(s_sqrt, b * 4 + u * 2 + n + 1)
                            dve.reciprocal(c[:, 2], c[:, 1]).then_inc(s_dve, 1)
                            count += 1
                            dve.wait_ge(s_dve, b * 2 * per + count)
                            dve.tensor_tensor(c[:, 3], c[:, 2], c[:, 2], ALU.mult).then_inc(s_dve, 1)
                            count += 1
                            dve.wait_ge(s_dve, b * 2 * per + count)
                            dve.tensor_tensor(c[:, 1], c[:, 3], c[:, 0], ALU.mult).then_inc(s_dve, 1)
                            count += 1
                            dve.wait_ge(s_dve, b * 2 * per + count)
                            dve.tensor_scalar(c[:, 3], c[:, 1], -0.5, 1.5, ALU.mult, ALU.add).then_inc(s_dve, 1)
                            count += 1
                            dve.wait_ge(s_dve, b * 2 * per + count)
                            dve.tensor_tensor(rstd[:, u, n], c[:, 3], c[:, 2], ALU.mult).then_inc(s_dve, 1)
                            count += 1
                            dve.wait_ge(s_dve, b * 2 * per + count)
                            if n == 1:
                                dve.wait_ge(s_yt, 2 * b + u - 1 if u else 2 * b)
                            for t in range(CH):
                                last = dve.tensor_scalar(dst[:, t], src[:, t], mv[:, u, n, t, 0:1], rstd[:, u, n, t:t + 1],
                                                         ALU.subtract, ALU.mult)
                            last.then_inc(s_dve if n == 0 else s_y, 1)
                            if n == 0:
                                count += 1
                                dve.wait_ge(s_dve, b * 2 * per + count)
                                dve.tensor_tensor(src, src, dst, ALU.add).then_inc(s_dve, 1)
                                count += 1
                        for a in range(2):
                            dve.wait_ge(s_p1, 4 * b + 2 * u + a + 1)
                            if a == 0:
                                dve.wait_ge(s_st[u], 16 * (2 + G) * b)
                            dve.tensor_tensor(rest[:, u, a], full[:, u, a], parts[:, u, a, 0], ALU.subtract).then_inc(s_dve, 1)
                            count += 1
                            dve.wait_ge(s_dve, b * 2 * per + count)
                            dve.tensor_copy(parts[:, u, a, 1], rest[:, u, a]).then_inc(s_dve, 1)
                            count += 1
                            dve.wait_ge(s_dve, b * 2 * per + count)
                            dve.tensor_tensor(parts[:, u, a, 2], rest[:, u, a], parts[:, u, a, 1], ALU.subtract).then_inc(s_split, 1)
                    assert count == 2 * per - 1 or count == 2 * per, (count, per)
                    while count < 2 * per:
                        dve.sem_inc(s_dve, 1)
                        count += 1

            @block.tensor
            def _(pe):
                pe.wait_ge(s_wp, 2)
                with pe.Fori(0, B) as b:
                    for u in range(2):
                        pe.wait_ge(s_y, 2 * b + u + 1)
                        pe.wait_ge(s_yT, 2 * b + u - 1 if u else 2 * b)
                        for t in range(CH):
                            last = pe.transpose(psum[:, u, t * P:(t + 1) * P], y[:, u, t], ident[:])
                        last.then_inc(s_yt, 1)
                        pe.wait_ge(s_yT, 2 * b + u + 1)
                        pe.wait_ge(s_p1, 4 * b + 2 * u)
                        pe.matmul(psum[:, 2], wq_s[:], yT[:, u], start=True, stop=True).then_inc(s_q, 1)
                        pe.matmul(psum[:, 3], wk_s[:], yT[:, u], start=True, stop=True).then_inc(s_k, 1)
                        pe.wait_ge(s_vw, 2 * b + u)
                        for t in range(CH):
                            last = pe.matmul(psum[:, 4, t * P:(t + 1) * P], yT[:, u, t * P:(t + 1) * P], wv_s[:], start=True, stop=True)
                        last.then_inc(s_v, 1)

            @block.scalar
            def _(act):
                act.wait_ge(s_w, 80)
                act.wait_ge(s_vinit, 4)
                with act.Fori(0, B) as b:
                    for u in range(2):
                        for n in range(2):
                            act.wait_ge(s_var, 4 * b + 2 * u + n + 1)
                            act.activation(tmp[:, u, n, 1], tmp[:, u, n, 0], ACT.Sqrt).then_inc(s_sqrt, 1)
                        act.wait_ge(s_yt, 2 * b + u + 1)
                        act.activation(yT[:, u], psum[:, u], ACT.Identity, bias=shift[:], scale=gain[:]).then_inc(s_yT, 1)
                        for a, s in ((0, s_q), (1, s_k)):
                            act.wait_ge(s, 2 * b + u + 1)
                            if a == 0:
                                act.wait_ge(s_st[u], 16 * (2 + G) * b)
                                act.wait_ge(s_split, 4 * b + (2 * u - 2 if u else 0))
                            scale = QSCALE if a == 0 else 1.0
                            act.activation(full[:, u, a], psum[:, 2 + a], ACT.Copy, scale=scale)
                            act.activation(parts[:, u, a, 0], psum[:, 2 + a], ACT.Copy, scale=scale).then_inc(s_p1, 1)
                        act.wait_ge(s_v, 2 * b + u + 1)
                        act.activation(vwin[:, u, :, 0:H * VW].rearrange("p t (h v) -> p t h v", v=VW)[:, :, :, 0:HD],
                                       psum[:, 4].rearrange("p (t h e) -> p t h e", t=CH, h=H), ACT.Copy).then_inc(s_vw, 1)


def attention(nc, octx, sem, L):
    (identb, ident, psum, qd, kd, vd, attn) = (L[n] for n in "identb ident psum qd kd vd attn".split())
    B, S, D, H, HD, HG, G, T, VW, VWIN, STACK = (L[n] for n in "B S D H HD HG G T VW VWIN STACK".split())
    rounds, leads, after, NR, NL, NU, AHEAD, PRO, diag, PER = (
        L[n] for n in "rounds leads after NR NL NU AHEAD PRO diag PER".split())
    STEPS = B * G
    PRO_UNITS = len(PRO) - 1
    NC = NR * HG
    HQ = 512
    TURN = leads.index(None)
    whole = T // 2

    def row_buf(g, n):
        return (g * NL + n) % ROWS

    def row_user(b, g, n):
        e = g * NL + n - ROWS
        if e < 0:
            last = {0: 0, 1: -2, 2: -1}[n]
            return s_max, PRO_UNITS + b * G * NU + last
        gg, nn = divmod(e, NL)
        i = b * G + gg
        if nn == TURN:
            return s_mrow, i + 2
        return s_max, PRO_UNITS + i * NU + nn + (nn < TURN)
    mturn_at = [n for n, a in enumerate(after) if leads.index(None) in a][0]
    with ExitStack() as ctx:
        def sb(name, shape, dt=F32):
            return ctx.enter_context(nc.sbuf_tensor(name, shape, dt))

        QS = sb("QS", [P, G, HG, S], BF16)
        KS = sb("KS", [P, G, HG, S], BF16)
        VS = sb("VS", [P, G, T, VWIN])
        probs = sb("probs", [P, 4, HG, HQ])
        causal = sb("causal", [P, 512])
        rowmax = sb("rowmax", [P, 2, T, HG])
        left = sb("left", [P, 2, 2, T, HG])
        firstmax = sb("firstmax", [P, 2, T // 2, HG])
        negm = sb("negm", [P, 2, T, PARTS, HG], BF16)
        mrow = sb("mrow", [PARTS * HG, 2, S], BF16)
        osum = sb("osum", [P, 2, HQ])
        rden = sb("rden", [P, 2, HQ // P, HG])

        rows = [psum[:, i] for i in range(ROWS)]
        cols = [psum[:, ROWS + i] for i in range(COLS)]
        outs = [psum[:, 6], psum[:, 7]]

        s_init = sem("s_init")
        s_passed_dve = sem("s_passed_dve")
        s_passed_pool = sem("s_passed_pool")
        s_ld = [sem(f"s_load{g}") for g in range(G)]
        s_ml = [sem(f"s_mload{g}") for g in range(G)]
        s_rows = sem("s_rows")
        s_max = sem("s_max")
        s_pool = sem("s_pool")
        s_whole = sem("s_whole")
        s_negm = sem("s_negm")
        s_mturn = sem("s_mturn")
        s_mrow = sem("s_mrow")
        s_cols = sem("s_cols")
        s_exp = sem("s_exp")
        s_mask = sem("s_mask")
        s_pv = sem("s_pv")
        s_oevac = [sem("s_oevac0"), sem("s_oevac1")]
        s_oturn = [sem("s_oturn0"), sem("s_oturn1")]
        s_rden = sem("s_rden")
        s_norm = [sem("s_norm0"), sem("s_norm1")]
        NLD = 2 * PARTS + 1

        def plus(b, g):
            return b + g // G, g % G

        with nc.Block() as block:
            @block.sync
            def _(sp):
                sp.wait_ge(s_init, 4)

                def load(b, g):
                    own = slice(g * HG * HD, (g + 1) * HG * HD)
                    for i in range(PARTS):
                        at = slice(i * PARTS * HD, (i + 1) * PARTS * HD)
                        q_i = qd[b, i, own, :].rearrange("(e h) t -> e (h t)", h=HG)
                        sp.dma_start(QS[at, g].rearrange("p h t -> p (h t)"),
                                     q_i.unsqueeze(0).broadcast_to([PARTS, HD, HG * S])).then_inc(s_ld[g], 16)
                        sp.dma_start(KS[at, g].rearrange("p h t -> p (h t)"),
                                     kd[b, :, own, :].rearrange("j (e h) t -> j e (h t)", h=HG)).then_inc(s_ld[g], 16)
                    sp.dma_start(VS[:, g], vd[b, g]).then_inc(s_ld[g], 16)

                def load_maxima(b, g):
                    sp.wait_ge(s_mrow, G * b + g + 1)
                    for i in range(PARTS):
                        sp.dma_start(QS[STACK + i:STACK + i + 1, g], mrow[i * HG:(i + 1) * HG, g % 2]).then_inc(s_ml[g], 16)

                def step(b, g, left_groups):
                    if left_groups > 3:
                        sp.wait_ge(s_pv, (b * G + g) * NR)
                        load(*plus(b, g + 3))
                    if left_groups > 1:
                        load_maxima(*plus(b, g + 1))

                for g in range(3):
                    load(0, g)
                load_maxima(0, 0)
                with sp.Fori(0, B - 1) as b:
                    for g in range(G):
                        step(b, g, G)
                for g in range(G):
                    step(B - 1, g, G - g)

            @block.gpsimd
            def _(pool):
                pool.memset(QS[64:P].rearrange("p g h t -> p (g h t)"), 0.0).then_inc(s_init, 1)
                pool.memset(KS[64:P].rearrange("p g h t -> p (g h t)"), 1.0).then_inc(s_init, 1)
                pool.wait_ge(s_init, 2)
                pool.memset(causal[:], 0.0).then_inc(s_init, 1)
                pool.wait_ge(s_init, 3)
                pool.affine_select(out=causal[:, 512 - P:], in_=causal[:, 512 - P:], compare_op=ALU.is_ge, fill=MASKED,
                                   base=0, pattern=[[-1, P]], channel_multiplier=1).then_inc(s_init, 1)

                def split_maxima(b, g):
                    i, w = G * b + g, g % 2
                    m, l, n = rowmax[:, w], left[:, w], negm[:, w]
                    wait_apart(pool, s_whole, i + 1, s_passed_pool)
                    if not isinstance(i, int) or i >= 2:
                        wait_apart(pool, s_mturn, i - 1, s_passed_pool)
                    pool.tensor_scalar(n[:, :, 0], m, -1.0, None, ALU.mult).then_inc(s_pool, 1)
                    wait_apart(pool, s_pool, 4 * i + 1, s_passed_pool)
                    pool.tensor_tensor(l[:, 0], m, n[:, :, 0], ALU.add).then_inc(s_pool, 1)
                    wait_apart(pool, s_pool, 4 * i + 2, s_passed_pool)
                    pool.tensor_scalar(n[:, :, 1], l[:, 0], -1.0, None, ALU.mult).then_inc(s_pool, 1)
                    wait_apart(pool, s_pool, 4 * i + 3, s_passed_pool)
                    pool.tensor_tensor(l[:, 1], l[:, 0], n[:, :, 1], ALU.add).then_inc(s_pool, 1)
                    wait_apart(pool, s_pool, 4 * i + 4, s_passed_pool)
                    pool.tensor_scalar(n[:, :, 2], l[:, 1], -1.0, None, ALU.mult).then_inc(s_negm, 1)

                def step(b, g, left_groups):
                    i = b * G + g
                    masks = [r for r in range(AHEAD, NR)] + [NR + r for r in range(AHEAD)]
                    for n, r in enumerate(masks):
                        if r % NR in diag and (r < NR or left_groups > 1):
                            mask(i + r // NR, r % NR)
                        if n == 3 and left_groups > 1:
                            split_maxima(*plus(b, g + 1))

                def mask(i, r):
                    wait_apart(pool, s_exp, (i * NR + r + 1) * HG, s_passed_pool)
                    tri = probs[:, r % 4, :, 0:P]
                    pool.affine_select(out=tri, in_=tri, compare_op=ALU.is_ge, fill=0.0, base=0,
                                       pattern=[[0, HG], [1, P]], channel_multiplier=-1).then_inc(s_mask, 1)

                split_maxima(0, 0)
                for r in range(AHEAD):
                    if r in diag:
                        mask(0, r)
                with pool.Fori(0, B - 1) as b:
                    for g in range(G):
                        step(b, g, G)
                for g in range(G):
                    step(B - 1, g, G - g)

            @block.tensor
            def _(pe):
                def lead(buf, b, g, h, qt, c, first, free):
                    if first:
                        pe.wait_ge(s_ld[g], 16 * NLD * (b + 1))
                    if free is not None:
                        pe.wait_ge(*free)
                    w = width(qt, c)
                    pe.matmul(rows[buf][:, 0:w], QS[0:STACK, g, h, qt * P:(qt + 1) * P],
                              KS[0:STACK, g, h, c * 512:c * 512 + w], start=True, stop=True).then_inc(s_rows, 1)

                def turn_maxima(buf, b, g, free):
                    pe.wait_ge(*free)
                    pe.wait_ge(s_negm, G * b + g + 1)
                    dst = rows[buf].bitcast(BF16)
                    for t in range(T):
                        last = pe.transpose(dst[0:PARTS * HG, t * P:(t + 1) * P],
                                            negm[:, g % 2, t].rearrange("p i h -> p (i h)"), identb[:])
                    last.then_inc(s_mturn, 1)

                def col(b, g, r, h):
                    i = b * G + g
                    qh, kt, q0, n = rounds[r]
                    if r == 0 and h == 0:
                        pe.wait_ge(s_ml[g], 16 * PARTS * (b + 1))
                    c = r * HG + h
                    if not isinstance(i, int) or i * NC + c >= COLS:
                        pe.wait_ge(s_exp, i * NC + c - COLS + 1)
                    pe.matmul(cols[c % COLS][:, 0:n], KS[:, g, h, kt * P:(kt + 1) * P], QS[:, g, h, q0:q0 + n],
                              start=True, stop=True).then_inc(s_cols, 1)

                def values(b, g, r):
                    i = b * G + g
                    qh, kt, q0, n = rounds[r]
                    if kt == 0:
                        pe.wait_ge(s_norm[qh], i)
                    if r in diag:
                        pe.wait_ge(s_mask, i * len(diag) + diag.index(r) + 1)
                    else:
                        pe.wait_ge(s_exp, (i * NR + r + 1) * HG)
                    last_kt = (qh + 1) * HQ // P - 1
                    for h in range(HG):
                        last = pe.matmul(outs[qh][32 * h:32 * h + 32, q0 - qh * HQ:HQ],
                                         VS[:, g, kt, h * VW:h * VW + 32], probs[:, r % 4, h, 0:n],
                                         start=(kt == 0), stop=(kt == last_kt), skip_group_check=True)
                    last.then_inc(s_pv, 1)

                def turn_out(b, g, qh):
                    pe.wait_ge(s_oevac[qh], b * G + g + 1)
                    for t in range(HQ // P):
                        last = pe.transpose(outs[qh][:, t * P:(t + 1) * P], osum[:, qh, t * P:(t + 1) * P], ident[:])
                    last.then_inc(s_oturn[qh], 1)

                def step(b, g, left_groups):
                    i = b * G + g
                    for k in range(NR):
                        values(b, g, k)
                        for h in range(HG):
                            r = k + AHEAD
                            if r < NR:
                                col(b, g, r, h)
                            elif left_groups > 1:
                                col(*plus(b, g + 1), r - NR, h)
                            for n in after[k * HG + h]:
                                x = leads[n]
                                ahead = 1 if x is None else x[0]
                                if left_groups <= ahead:
                                    continue
                                buf = row_buf(g, n)
                                if x is None:
                                    free = row_user(b, g, n) if left_groups > 2 else (s_max, PRO_UNITS + i * NU + PER)
                                    turn_maxima(buf, *plus(b, g + 1), free)
                                else:
                                    bb, gg = plus(b, g + x[0])
                                    lead(buf, bb, gg, *x[1:], n == PER, row_user(b, g, n))
                        if k >= 1 and rounds[k - 1][0] == 0 and rounds[k][0] == 1:
                            turn_out(b, g, 0)
                    turn_out(b, g, 1)

                pe.wait_ge(s_init, 4)
                turn = PRO.index(None)
                for n, x in enumerate(PRO):
                    free = None
                    if n >= ROWS:
                        before = n - ROWS
                        free = (s_mrow, 1) if before == turn else (s_max, before + (before < turn))
                    if x is None:
                        turn_maxima(n % ROWS, 0, 0, free)
                    else:
                        lead(n % ROWS, 0, *x, n % (HG * PER) == 0, free)
                for r in range(AHEAD):
                    for h in range(HG):
                        col(0, 0, r, h)
                with pe.Fori(0, B - 1) as b:
                    for g in range(G):
                        step(b, g, G)
                for g in range(G):
                    step(B - 1, g, G - g)

            @block.scalar
            def _(act):
                def exps(b, g, r, turn=None):
                    i = b * G + g
                    n = rounds[r][3]
                    R = i * NR + r
                    if not isinstance(i, int) or R >= 4:
                        act.wait_ge(s_pv, i * NR + max(r - 3, 0) if r >= AHEAD else R - 3)
                    for h in range(HG):
                        act.wait_ge(s_cols, R * HG + h + 1)
                        act.activation(probs[:, r % 4, h, 0:n], cols[(r * HG + h) % COLS][:, 0:n], ACT.Exp).then_inc(s_exp, 1)
                        if turn is not None and turn[0] == h:
                            maxima(*turn[1:])

                def evac(b, g, qh):
                    i = b * G + g
                    last = [r for r in range(NR) if rounds[r][0] == qh][-1]
                    act.wait_ge(s_pv, i * NR + last + 1)
                    act.activation(osum[:, qh], outs[qh], ACT.Copy).then_inc(s_oevac[qh], 1)

                def maxima(b, g, buf):
                    act.wait_ge(s_mturn, b * G + g + 1)
                    if g >= 2:
                        act.wait_ge(s_ml[g - 2], 16 * PARTS * (b + 1))
                    else:
                        act.wait_ge(s_ml[g + 2], 16 * PARTS * b)
                    act.activation(mrow[:, g % 2], rows[buf].bitcast(BF16)[0:PARTS * HG], ACT.Copy).then_inc(s_mrow, 1)

                def step(b, g, left_groups):
                    for k in range(NR):
                        r = k + AHEAD
                        turn = None
                        if k == mturn_at // HG and left_groups > 1:
                            turn = (mturn_at % HG, *plus(b, g + 1), row_buf(g, TURN))
                        if r < NR:
                            exps(b, g, r, turn)
                        elif left_groups > 1:
                            exps(*plus(b, g + 1), r - NR, turn)
                        if k >= 1 and rounds[k - 1][0] == 0 and rounds[k][0] == 1:
                            evac(b, g, 0)
                    evac(b, g, 1)

                maxima(0, 0, PRO.index(None) % ROWS)
                for r in range(AHEAD):
                    exps(0, 0, r)
                with act.Fori(0, B - 1) as b:
                    for g in range(G):
                        step(b, g, G)
                for g in range(G):
                    step(B - 1, g, G - g)

            @block.vector
            def _(dve):
                def maxima(buf, m, w, h, qt, c):
                    n = width(qt, c)
                    tile = rows[buf][:, 0:n]
                    if c * 512 + n == (qt + 1) * P:
                        wait_apart(dve, s_rows, m + 1, s_passed_dve)
                        dve.wait_ge(s_init, 4)
                        dve.tensor_tensor_reduce(tile, tile, causal[:, 512 - n:], 1.0, MASKED, ALU.add, ALU.max,
                                                 rowmax[:, w, qt, h:h + 1]).then_inc(s_max, 1)
                    else:
                        dve.wait_ge(s_rows, m + 1)
                        dve.reduce_max(firstmax[:, w, qt - whole, h:h + 1], tile, AX.X).then_inc(s_max, 1)

                def join(w, count):
                    dve.wait_ge(s_max, count)
                    m = rowmax[:, w, whole:]
                    dve.tensor_tensor(m, m, firstmax[:, w], ALU.max).then_inc(s_whole, 1)

                def norm(b, g, qh):
                    i = b * G + g
                    dve.wait_ge(s_oturn[qh], i + 1)
                    o = outs[qh].rearrange("p (t h v) -> p t h v", t=HQ // P, h=HG)
                    dve.reciprocal(rden[:, qh], o[:, :, :, HD]).then_inc(s_rden, 1)
                    dve.wait_ge(s_rden, 2 * i + qh + 1)
                    nt = HQ // P
                    dst = attn[:, b, qh * nt:(qh + 1) * nt, g * HG * HD:(g + 1) * HG * HD].rearrange("p t (h e) -> p t h e", h=HG)
                    dve.tensor_tensor(dst, o[:, :, :, 0:HD], rden[:, qh].unsqueeze(3).broadcast_to([P, nt, HG, HD]),
                                      ALU.mult).then_inc(s_norm[qh], 1)

                def step(b, g, left_groups):
                    i = b * G + g
                    units = PRO_UNITS + i * NU
                    for k in range(NR):
                        for h in range(HG):
                            for n in after[k * HG + h]:
                                x = leads[n]
                                if left_groups == 2 and n == PER + 1:
                                    join((g + 1) % 2, units + PER)
                                if x is None or left_groups <= x[0]:
                                    continue
                                done = sum(1 for e in leads[:n] if e is not None)
                                gg = (g + x[0]) % G
                                maxima(row_buf(g, n), units + done, gg % 2, *x[1:])
                                if n == PER + 1:
                                    join((g + 1) % 2, units + PER)
                        if k >= 1 and rounds[k - 1][0] == 0 and rounds[k][0] == 1:
                            norm(b, g, 0)
                    norm(b, g, 1)

                m = 0
                for n, x in enumerate(PRO):
                    if x is not None:
                        maxima(n % ROWS, m, x[0] % 2, *x[1:])
                        m += 1
                    if n == HG * PER + 1:
                        join(0, HG * PER)
                with dve.Fori(0, B - 1) as b:
                    for g in range(G):
                        step(b, g, G)
                for g in range(G):
                    step(B - 1, g, G - g)


def project(nc, octx, sem, L):
    (attn, tokens, ident, psum, rowbuf, xnT, logits, wo, rw, rb) = (
        L[n] for n in "attn tokens ident psum rowbuf xnT logits wo rw rb".split())
    B, S, D, G, T, CH, E, ROW = (L[n] for n in "B S D G T CH E ROW".split())
    W = CH * P
    with ExitStack() as ctx:
        def sb(name, shape, dt=F32):
            return ctx.enter_context(nc.sbuf_tensor(name, shape, dt))

        wo_s = sb("wo_s", [P, D])
        rwT = sb("rwT", [D, E])
        rb_s = sb("rb_s", [P, E])
        a_in = sb("a_in", [P, 2, CH, D])
        aT = sb("aT", [P, 2, W])
        stat = sb("stat2", [P, 2, CH, 6])
        mv = sb("mv2", [P, 2, CH, 2])
        rstd = sb("rstd2", [P, 2, CH])
        tmp = sb("tmp2", [P, 2, 4, CH])
        y = sb("xn", [P, 2, CH, D])
        yT = sb("xnTc", [D, 2, W])

        s_w = sem("s_w2")
        s_passed = sem("s_passed_project")
        s_a = sem("s_a")
        s_at = sem("s_at")
        s_aT = sem("s_aT")
        s_o = sem("s_o")
        s_x1 = sem("s_resid")
        s_dve = sem("s_dve2")
        s_var = sem("s_var2")
        s_sqrt = sem("s_sqrt2")
        s_y = sem("s_y2")
        s_yt = sem("s_yt2")
        s_yT = sem("s_yT2")
        s_row = sem("s_row")
        s_lg = sem("s_lg")
        s_lgd = sem("s_lgd")

        with nc.Block() as block:
            @block.sync
            def _(sp):
                sp.dma_start(wo_s[:], wo).then_inc(s_w, 16)
                sp.dma_start(rwT[:], rw.rearrange("e d -> d e"), allow_slow_non_contiguous=True).then_inc(s_w, 16)
                sp.dma_start(rb_s[:], rb.partition_broadcast(P)).then_inc(s_w, 16)

            @block.gpsimd
            def _(pool):
                pool.iota(rowbuf[:, :, :, 2 * D:].bitcast(U32), pattern=[[S, B], [P, T], [1, 1]], base=0,
                          channel_multiplier=1)
                with pool.Fori(0, B) as b:
                    for u in range(2):
                        pool.wait_ge(s_y, 2 * b + u + 1)
                        pool.tensor_copy(rowbuf[:, b, u * CH:(u + 1) * CH, 0:D], y[:, u]).then_inc(s_row, 1)

            @block.vector
            def _(dve):
                dve.wait_ge(s_w, 48)
                per = 7
                with dve.Fori(0, B) as b:
                    count = 0
                    for u in range(2):
                        def fence():
                            dve.wait_ge(s_dve, b * 2 * per + count)

                        x1 = rowbuf[:, b, u * CH:(u + 1) * CH, D:2 * D]
                        dve.wait_ge(s_o, 2 * b + u + 1)
                        dve.tensor_tensor(x1, tokens[:, b, u * CH:(u + 1) * CH],
                                          psum[:, 2].rearrange("p (t d) -> p t d", t=CH), ALU.add).then_inc(s_x1, 1)
                        wait_apart(dve, s_x1, 2 * b + u + 1, s_passed)
                        for t in range(CH):
                            last = dve.bn_stats(stat[:, u, t], x1[:, t])
                        last.then_inc(s_dve, 1)
                        count += 1
                        wait_apart(dve, s_dve, b * 2 * per + count, s_passed)
                        for t in range(CH):
                            last = dve.bn_aggr(mv[:, u, t], stat[:, u, t:t + 1])
                        last.then_inc(s_dve, 1)
                        count += 1
                        fence()
                        c = tmp[:, u]
                        dve.tensor_scalar(c[:, 0], mv[:, u, :, 1], EPS, None, ALU.add).then_inc(s_var, 1)
                        dve.wait_ge(s_sqrt, 2 * b + u + 1)
                        dve.reciprocal(c[:, 2], c[:, 1]).then_inc(s_dve, 1)
                        count += 1
                        fence()
                        dve.tensor_tensor(c[:, 3], c[:, 2], c[:, 2], ALU.mult).then_inc(s_dve, 1)
                        count += 1
                        fence()
                        dve.tensor_tensor(c[:, 1], c[:, 3], c[:, 0], ALU.mult).then_inc(s_dve, 1)
                        count += 1
                        fence()
                        dve.tensor_scalar(c[:, 3], c[:, 1], -0.5, 1.5, ALU.mult, ALU.add).then_inc(s_dve, 1)
                        count += 1
                        fence()
                        dve.tensor_tensor(rstd[:, u], c[:, 3], c[:, 2], ALU.mult).then_inc(s_dve, 1)
                        count += 1
                        fence()
                        dve.wait_ge(s_yt, 2 * b + u - 1 if u else 2 * b)
                        dve.wait_ge(s_row, 2 * b + u - 1 if u else 2 * b)
                        for t in range(CH):
                            last = dve.tensor_scalar(y[:, u, t], x1[:, t], mv[:, u, t, 0:1], rstd[:, u, t:t + 1],
                                                     ALU.subtract, ALU.mult)
                        last.then_inc(s_y, 1)
                        dve.wait_ge(s_lg, 2 * b + u + 1)
                        dve.tensor_tensor(logits[:, :, b, u * CH:(u + 1) * CH].rearrange("p e t -> p t e"),
                                          psum[:, 6, 0:CH * E].rearrange("p (t e) -> p t e", t=CH),
                                          rb_s[:].unsqueeze(1).broadcast_to([P, CH, E]), ALU.add).then_inc(s_lgd, 1)
                    assert count == 2 * per

            @block.tensor
            def _(pe):
                pe.wait_ge(s_w, 48)
                with pe.Fori(0, B) as b:
                    for u in range(2):
                        pe.wait_ge(s_a, 2 * b + u + 1)
                        pe.wait_ge(s_aT, 2 * b + u - 1 if u else 2 * b)
                        for t in range(CH):
                            last = pe.transpose(psum[:, u, t * P:(t + 1) * P], a_in[:, u, t], ident[:])
                        last.then_inc(s_at, 1)
                        pe.wait_ge(s_aT, 2 * b + u + 1)
                        pe.wait_ge(s_x1, 2 * b + u)
                        for t in range(CH):
                            last = pe.matmul(psum[:, 2, t * P:(t + 1) * P], aT[:, u, t * P:(t + 1) * P], wo_s[:], start=True, stop=True)
                        last.then_inc(s_o, 1)
                        pe.wait_ge(s_y, 2 * b + u + 1)
                        pe.wait_ge(s_yT, 2 * b + u - 1 if u else 2 * b)
                        for t in range(CH):
                            last = pe.transpose(psum[:, 4 + u, t * P:(t + 1) * P], y[:, u, t], ident[:])
                        last.then_inc(s_yt, 1)
                        pe.wait_ge(s_yT, 2 * b + u + 1)
                        pe.wait_ge(s_lgd, 2 * b + u)
                        for t in range(CH):
                            last = pe.matmul(psum[:, 6, t * E:(t + 1) * E], yT[:, u, t * P:(t + 1) * P], rwT[:], start=True, stop=True)
                        last.then_inc(s_lg, 1)

            @block.scalar
            def _(act):
                with act.Fori(0, B) as b:
                    for u in range(2):
                        act.wait_ge(s_at, 2 * b + u - 1 if u else 2 * b)
                        act.activation(a_in[:, u], attn[:, b, u * CH:(u + 1) * CH], ACT.Copy).then_inc(s_a, 1)
                        act.wait_ge(s_at, 2 * b + u + 1)
                        act.wait_ge(s_o, 2 * b + u - 1 if u else 2 * b)
                        act.activation(aT[:, u], psum[:, u], ACT.Copy).then_inc(s_aT, 1)
                        act.wait_ge(s_var, 2 * b + u + 1)
                        act.activation(tmp[:, u, 1], tmp[:, u, 0], ACT.Sqrt).then_inc(s_sqrt, 1)
                        act.wait_ge(s_yt, 2 * b + u + 1)
                        act.wait_ge(s_lg, 2 * b + u - 1 if u else 2 * b)
                        act.activation(xnT[:, b, u * W:(u + 1) * W], psum[:, 4 + u], ACT.Copy)
                        act.activation(yT[:, u], psum[:, 4 + u], ACT.Copy).then_inc(s_yT, 1)


def route(nc, octx, sem, L):
    (psum, rowbuf, logits, slot, sorted_rows) = (L[n] for n in "psum rowbuf logits slot sorted_rows".split())
    N, NT, E, CAP, ROW, D = (L[n] for n in "N NT E CAP ROW D".split())
    with ExitStack() as ctx:
        def sb(name, shape, dt=F32):
            return ctx.enter_context(nc.sbuf_tensor(name, shape, dt))

        before = sb("before", [P, P], BF16)
        ones = sb("ones", [P, P], BF16)
        rank = sb("rank", [P, E, NT])
        base = sb("base", [P, E, NT])
        fresh = sb("fresh", [P, E, NT])
        own_row = sb("own_row", [P, NT])
        empty = sb("empty", [P, ROW])
        iw = sb("iw", [P, E, NT], mybir.dt.int32)
        bufs = {n: sb(n, [P, E, NT]) for n in "gate pick weigh pos1 pos2 incl one two prod".split()}
        gate, pick, weigh, pos1, pos2, incl, one, two, prod = bufs.values()
        oneb, twob = sb("oneb", [P, E, NT], BF16), sb("twob", [P, E, NT], BF16)
        small = sb("small", [P, 12, NT])
        used = sb("used", [P, E])

        s_fill = sem("s_fill")
        s_c = sem("s_c")
        s_dve = sem("s_dve3")
        s_exp = sem("s_exp3")
        s_one, s_cum = sem("s_one"), sem("s_cum")
        s_slot = sem("s_slot")
        s_sc = sem("s_scatter")
        flat = "p e t -> p (e t)"

        with nc.Block() as block:
            @block.sync
            def _(sp):
                sp.wait_ge(s_c, 8)
                sp.dma_start(sorted_rows[0:E * CAP].rearrange("(t p) c -> p t c", p=P),
                             empty[:].unsqueeze(1).broadcast_to([P, E * CAP // P, ROW])).then_inc(s_fill, 16)

            @block.gpsimd
            def _(pool):
                count = [0]

                def own(ins):
                    ins.then_inc(s_c, 1)
                    count[0] += 1
                    pool.wait_ge(s_c, count[0])

                own(pool.memset(before[:], 1.0))
                own(pool.affine_select(out=before[:], in_=before[:], compare_op=ALU.is_gt, fill=0.0, base=0,
                                       pattern=[[1, P]], channel_multiplier=-1))
                own(pool.memset(ones[:], 1.0))
                own(pool.iota(rank[:], pattern=[[-1, E], [0, NT]], base=E, channel_multiplier=0,
                              allow_small_or_imprecise_dtypes=True))
                own(pool.iota(base[:], pattern=[[CAP, E], [0, NT]], base=0, channel_multiplier=0,
                              allow_small_or_imprecise_dtypes=True))
                own(pool.iota(own_row[:], pattern=[[P, NT]], base=E * CAP, channel_multiplier=1,
                              allow_small_or_imprecise_dtypes=True))
                own(pool.memset(empty[:, 0:2 * D], 0.0))
                own(pool.memset(empty[:, 2 * D:].bitcast(U32), N))
                own(pool.memset(fresh[:], 1.0))
                own(pool.memset(fresh[:, :, 0:1], 0.0))
                pool.wait_ge(s_fill, 16)
                pool.wait_ge(s_slot, 1)
                for t in range(NT):
                    pool.indirect_dma_start(out=sorted_rows, out_offset=bass.IndirectOffsetOnAxis(ap=slot[:, t:t + 1], axis=0),
                                            in_=rowbuf[:].rearrange("p b t c -> p (b t) c")[:, t], in_offset=None).then_inc(s_sc, 16)
                pool.wait_ge(s_sc, 16 * NT)

            @block.scalar
            def _(act):
                act.wait_ge(s_dve, 2)
                act.activation(pick[:], gate[:], ACT.Exp).then_inc(s_exp, 1)

            @block.tensor
            def _(pe):
                pe.wait_ge(s_c, 3)
                for n, sel in enumerate((oneb, twob)):
                    pe.wait_ge(s_one, n + 1)
                    pe.matmul(psum[:, 2 * n, 0:E * NT], before[:], sel[:].rearrange(flat), start=True, stop=True)
                    pe.matmul(psum[:, 2 * n + 1, 0:E * NT], ones[:], sel[:].rearrange(flat), start=True, stop=True).then_inc(s_cum, 1)

            @block.vector
            def _(dve):
                count = [0]

                def own(ins):
                    ins.then_inc(s_dve, 1)
                    count[0] += 1
                    dve.wait_ge(s_dve, count[0])

                def by_token(ap):
                    return ap.rearrange("p e t -> p t e")

                def wide(ap):
                    return ap.unsqueeze(1).broadcast_to([P, E, NT])

                def choose(src, best, hot):
                    own(dve.reduce_max(best, by_token(src), AX.X))
                    own(dve.tensor_tensor(weigh[:], src, wide(best), ALU.is_equal))
                    own(dve.tensor_tensor(weigh[:], weigh[:], rank[:], ALU.mult))
                    own(dve.reduce_max(best, by_token(weigh[:]), AX.X))
                    own(dve.tensor_tensor(hot, weigh[:], wide(best), ALU.is_equal))

                def places(n, pos):
                    dve.wait_ge(s_cum, n + 1)
                    total = psum[:, 2 * n + 1, 0:E * NT]
                    own(dve.tensor_tensor_scan(incl[:].rearrange(flat), fresh[:].rearrange(flat), total, 0.0,
                                               ALU.mult, ALU.add))
                    own(dve.tensor_tensor(pos, incl[:], total.rearrange("p (e t) -> p e t", e=E), ALU.subtract))
                    own(dve.tensor_tensor(pos, pos, psum[:, 2 * n, 0:E * NT].rearrange("p (e t) -> p e t", e=E), ALU.add))

                def at(hot, src, dst):
                    own(dve.tensor_tensor(prod[:], hot, src, ALU.mult))
                    own(dve.reduce_sum(dst, by_token(prod[:]), AX.X))

                k = [small[:, i] for i in range(12)]
                lg = logits[:].rearrange("p e b t -> p e (b t)")
                own(dve.reduce_max(k[0], by_token(lg), AX.X))
                own(dve.tensor_tensor(gate[:], lg, wide(k[0]), ALU.subtract))
                dve.wait_ge(s_exp, 1)
                own(dve.reduce_sum(k[0], by_token(pick[:]), AX.X))
                own(dve.reciprocal(k[1], k[0]))
                own(dve.tensor_tensor(gate[:], pick[:], wide(k[1]), ALU.mult))
                dve.wait_ge(s_c, 10)
                choose(gate[:], k[0], one[:])
                dve.tensor_copy(oneb[:], one[:]).then_inc(s_one, 1)
                own(dve.scalar_tensor_tensor(out=gate[:], in0=one[:], scalar=-2.0, in1=gate[:], op0=ALU.mult, op1=ALU.add))
                choose(gate[:], k[0], two[:])
                places(0, pos1[:])
                own(dve.tensor_scalar(used[:], incl[:, :, NT - 1], float(CAP), None, ALU.min))
                at(one[:], pos1[:], k[1])
                at(one[:], base[:], k[2])
                own(dve.tensor_scalar(k[3], k[1], float(CAP), None, ALU.is_lt))
                own(dve.tensor_scalar(k[4], k[3], -1.0, 1.0, ALU.mult, ALU.add))
                own(dve.tensor_tensor(prod[:], two[:], wide(k[4]), ALU.mult))
                dve.tensor_copy(twob[:], prod[:]).then_inc(s_one, 1)
                own(dve.tensor_tensor(k[5], k[1], k[2], ALU.add))
                places(1, pos2[:])
                own(dve.tensor_tensor(pos2[:], pos2[:], used[:].unsqueeze(2).broadcast_to([P, E, NT]), ALU.add))
                at(two[:], pos2[:], k[6])
                at(two[:], base[:], k[7])
                own(dve.tensor_scalar(k[8], k[6], float(CAP), None, ALU.is_lt))
                own(dve.tensor_tensor(k[8], k[8], k[4], ALU.mult))
                own(dve.tensor_tensor(k[9], k[6], k[7], ALU.add))
                own(dve.tensor_tensor(k[10], k[4], k[8], ALU.subtract))
                own(dve.tensor_tensor(k[5], k[5], k[3], ALU.mult))
                own(dve.tensor_tensor(k[9], k[9], k[8], ALU.mult))
                own(dve.tensor_tensor(k[10], k[10], own_row[:], ALU.mult))
                own(dve.tensor_tensor(k[5], k[5], k[9], ALU.add))
                own(dve.tensor_tensor(k[5], k[5], k[10], ALU.add))
                dve.tensor_copy(slot[:], k[5]).then_inc(s_slot, 1)


def experts(nc, octx, sem, L):
    (psum, ident, rowbuf, xnT, sorted_rows, w1, b1, w2, b2, sw1, sb1, sw2, sb2, out) = (
        L[n] for n in "psum ident rowbuf xnT sorted_rows w1 b1 w2 b2 sw1 sb1 sw2 sb2 out".split())
    B, N, S, NT, E, CAP, ROW, D, F, FC, CH = (L[n] for n in "B N S NT E CAP ROW D F FC CH".split())
    W = CH * P
    assert CAP == W and S == 2 * W
    with ExitStack() as ctx:
        def sb(name, shape, dt=F32):
            return ctx.enter_context(nc.sbuf_tensor(name, shape, dt))

        sw1_s, sw2_s = sb("sw1_s", [D, F]), sb("sw2_s", [P, FC, D])
        sb1_s, sb2_s = sb("sb1_s", [P, FC]), sb("sb2_s", [P, D])
        w1_s, w2_s = sb("w1_s", [D, 2, F]), sb("w2_s", [P, 2, FC, D])
        b1_s, b2_s = sb("b1_s", [P, E, FC]), sb("b2_s", [P, E, D])
        xs = sb("xs", [P, 2, CH, ROW])
        xsT = sb("xsT", [D, 2, W])
        hid = sb("hid", [P, 2, FC, W])
        res = sb("res", [P, 2, CH, D])

        s_sw = sem("s_sw")
        s_passed = sem("s_passed_experts")
        s_ew = [sem("s_ew0"), sem("s_ew1")]
        s_xs = [sem("s_xs0"), sem("s_xs1")]
        s_h, s_g, s_yy, s_add, s_res = sem("s_h"), sem("s_g"), sem("s_yy"), sem("s_add"), sem("s_res")
        s_xt, s_xT = sem("s_xt"), sem("s_xT")
        s_out = [sem("s_out0"), sem("s_out1")]
        s_fin = sem("s_fin")
        s_dn = sem("s_dense")
        s_put = [sem("s_put0"), sem("s_put1")]
        JOBS = N // W

        with nc.Block() as block:
            @block.sync
            def _(sp):
                def weights(e, u):
                    sp.dma_start(w1_s[:, u], w1[e]).then_inc(s_ew[u], 16)
                    sp.dma_start(w2_s[:, u], w2[e].rearrange("(c p) d -> p c d", p=P)).then_inc(s_ew[u], 16)

                def rows_of(e, u):
                    sp.dma_start(xs[:, u], sorted_rows.rearrange("(k t p) c -> k p t c", t=CH, p=P)[e]).then_inc(s_xs[u], 16)

                sp.dma_start(sw1_s[:], sw1).then_inc(s_sw, 16)
                sp.dma_start(sw2_s[:], sw2.rearrange("(c p) d -> p c d", p=P)).then_inc(s_sw, 16)
                sp.dma_start(sb1_s[:], sb1.rearrange("(c p) -> p c", p=P), allow_slow_non_contiguous=True).then_inc(s_sw, 16)
                sp.dma_start(sb2_s[:], sb2.partition_broadcast(P)).then_inc(s_sw, 16)
                sp.dma_start(b1_s[:], b1.rearrange("e (c p) -> p e c", p=P), allow_slow_non_contiguous=True).then_inc(s_sw, 16)
                sp.dma_start(b2_s[:], b2.partition_broadcast(P)).then_inc(s_sw, 16)
                for u in range(2):
                    weights(u, u)
                    rows_of(u, u)
                with sp.Fori(0, B) as b:
                    for u in range(2):
                        sp.wait_ge(s_res, 2 * b + u + 1)
                        sp.dma_start(out[b].rearrange("(k t p) d -> k p t d", k=2, p=P)[u], res[:, u]).then_inc(s_out[u], 16)
                for u in range(2):
                    sp.wait_ge(s_out[u], 16 * B)
                sp.nop().then_inc(s_dn, 1)
                with sp.Fori(0, E // 2 - 1) as k:
                    for u in range(2):
                        sp.wait_ge(s_yy, JOBS + 2 * k + u + 1)
                        weights(2 * k + u + 2, u)
                        sp.wait_ge(s_put[u], 16 * CH * (k + 1))
                        rows_of(2 * k + u + 2, u)

            @block.gpsimd
            def _(pool):
                pool.wait_ge(s_dn, 1)
                last_token = pool.to_reg(N - 1)
                with pool.Fori(0, E // 2) as k:
                    for u in range(2):
                        for t in range(CH):
                            if t == 0:
                                wait_apart(pool, s_res, JOBS + 2 * k + u + 1, s_passed)
                            pool.indirect_dma_start(
                                out=out.rearrange("b s d -> (b s) d"),
                                out_offset=bass.IndirectOffsetOnAxis(ap=xs[:, u, t, 2 * D:].bitcast(U32), axis=0),
                                in_=res[:, u, t], in_offset=None, bounds_check=last_token, oob_is_err=False).then_inc(s_put[u], 16)
                for u in range(2):
                    pool.wait_ge(s_put[u], 16 * CH * (E // 2))

            @block.tensor
            def _(pe):
                def up(j, u, w, x):
                    for c in range(FC):
                        pe.wait_ge(s_g, FC * j + c + 1 - FC if u else FC * j)
                        pe.matmul(psum[:, c], w[:, c * P:(c + 1) * P], x, start=True, stop=True).then_inc(s_h, 1)

                def down(j, u, w):
                    pe.wait_ge(s_g, FC * (j + 1))
                    pe.wait_ge(s_add, j - 1 if u else j)
                    for t in range(CH):
                        for c in range(FC):
                            last = pe.matmul(psum[:, 4 + u, t * P:(t + 1) * P], hid[:, u, c, t * P:(t + 1) * P], w[:, c],
                                             start=(c == 0), stop=(c == FC - 1))
                    last.then_inc(s_yy, 1)

                pe.wait_ge(s_sw, 96)
                with pe.Fori(0, B) as b:
                    for u in range(2):
                        up(2 * b + u, u, sw1_s, xnT[:, b, u * W:(u + 1) * W])
                    for u in range(2):
                        down(2 * b + u, u, sw2_s)
                with pe.Fori(0, E // 2) as k:
                    for u in range(2):
                        pe.wait_ge(s_xs[u], 16 * (k + 1))
                        pe.wait_ge(s_xT, 2 * k)
                        for t in range(CH):
                            last = pe.transpose(psum[:, 6 + u, t * P:(t + 1) * P], xs[:, u, t, 0:D], ident[:])
                        last.then_inc(s_xt, 1)
                    for u in range(2):
                        pe.wait_ge(s_ew[u], 32 * (k + 1))
                        pe.wait_ge(s_xT, 2 * k + u + 1)
                        up(JOBS + 2 * k + u, u, w1_s[:, u], xsT[:, u])
                    for u in range(2):
                        down(JOBS + 2 * k + u, u, w2_s[:, u])

            @block.scalar
            def _(act):
                def gelu(j, u, bias):
                    for c in range(FC):
                        act.wait_ge(s_h, FC * j + c + 1)
                        if c == 0:
                            act.wait_ge(s_yy, j - 1 if u else j)
                        act.activation(hid[:, u, c], psum[:, c], ACT.Gelu, bias=bias(c)).then_inc(s_g, 1)

                act.wait_ge(s_sw, 96)
                with act.Fori(0, B) as b:
                    for u in range(2):
                        gelu(2 * b + u, u, lambda c: sb1_s[:, c:c + 1])
                with act.Fori(0, E // 2) as k:
                    for u in range(2):
                        act.wait_ge(s_xt, 2 * k + u + 1)
                        act.activation(xsT[:, u], psum[:, 6 + u], ACT.Copy).then_inc(s_xT, 1)
                    for u in range(2):
                        gelu(JOBS + 2 * k + u, u, lambda c: b1_s[:, 2 * k + u, c:c + 1])

            @block.vector
            def _(dve):
                def finish(j, u, x1, bias, stored):
                    dve.wait_ge(s_yy, j + 1)
                    dve.wait_ge(*stored)
                    dve.tensor_tensor(res[:, u], x1, psum[:, 4 + u].rearrange("p (t d) -> p t d", t=CH), ALU.add).then_inc(s_add, 1)
                    dve.wait_ge(s_add, j + 1)
                    dve.tensor_tensor(res[:, u], res[:, u], bias.unsqueeze(1).broadcast_to([P, CH, D]), ALU.add).then_inc(s_res, 1)

                dve.wait_ge(s_sw, 96)
                with dve.Fori(0, B) as b:
                    for u in range(2):
                        finish(2 * b + u, u, rowbuf[:, b, u * CH:(u + 1) * CH, D:2 * D], sb2_s[:], (s_out[u], 16 * b))
                for u in range(2):
                    dve.wait_ge(s_out[u], 16 * B)
                with dve.Fori(0, E // 2) as k:
                    for u in range(2):
                        dve.wait_ge(s_xs[u], 16 * (k + 1))
                        finish(JOBS + 2 * k + u, u, xs[:, u, :, D:2 * D], b2_s[:, 2 * k + u], (s_put[u], 16 * CH * k))


_INS = ['L0_attn_x', 'L0_attn_ln_w', 'L0_attn_ln_b', 'L0_attn_wq', 'L0_attn_wk', 'L0_attn_wv', 'L0_attn_wo',
        'L0_ffn_rw', 'L0_ffn_rb', 'L0_ffn_w1', 'L0_ffn_b1', 'L0_ffn_w2', 'L0_ffn_b2', 'L0_ffn_sw1', 'L0_ffn_sb1',
        'L0_ffn_sw2', 'L0_ffn_sb2']
_OUTS = [((4, 1024, 128), 'float32')]


def kernel(**inputs):
    import numpy as _np
    import concourse.bacc as _bacc
    from concourse import mybir as _mybir
    from concourse.bass_utils import run_bass_kernel_spmd as _run

    nc = _bacc.Bacc("TRN2", target_bir_lowering=False, num_devices=1)
    arrays, args = {}, []
    for name in _INS:
        a = _np.ascontiguousarray(inputs[name])
        arrays[f"in_{name}_dram"] = a
        args.append(nc.dram_tensor(f"in_{name}_dram", a.shape, _mybir.dt.from_np(a.dtype), kind="ExternalInput").ap())
    for i, (shape, dtype) in enumerate(_OUTS):
        dt = _mybir.dt.from_np(_np.dtype(dtype))
        args.append(nc.dram_tensor(f"out_{i}_dram", shape, dt, kind="ExternalOutput").ap())
    build(nc, *args)
    r = _run(nc, [arrays], core_ids=[0])
    got = tuple(r.results[0][f"out_{i}_dram"] for i in range(len(_OUTS)))
    return got[0]
```

```python
from contextlib import ExitStack

import concourse.bass as bass
from concourse import mybir

ALU = mybir.AluOpType
ACT = mybir.ActivationFunctionType
AX = mybir.AxisListType
F32 = mybir.dt.float32
BF16 = mybir.dt.bfloat16
U32 = mybir.dt.uint32

P = 128
PARTS = 3
TERMS = PARTS * PARTS
MASKED = -3.0e38
EPS = 1e-5
TWO_ONES = 0x3F803F80
AHEAD = 2
LEAD = 3
SHARES = (2, 1, 0, 1)
TURN_LAG = 9
ROWS = 3
COLS = 3
BUFS = 4


def attention_plan(S, HG):
    tiles = S // P
    half = 512
    rounds = []
    for qh in range(S // half):
        for kt in range((qh + 1) * half // P):
            q0 = max(qh * half, kt * P)
            rounds.append((qh, kt, q0, (qh + 1) * half - q0))
    last = [(qt, qt * P // half) for qt in range(tiles)]
    whole = [(qt, c) for qt in reversed(range(tiles)) for c in range(qt * P // half)]
    last.sort(key=lambda x: x[0] * P % half)
    order, wide = [], whole + last[len(last) - (len(last) - len(whole)) // 2:]
    narrow = last[:len(last) - (len(last) - len(whole)) // 2]
    while wide or narrow:
        order += wide[:1] + narrow[:1]
        wide, narrow = wide[1:], narrow[1:]
    per = len(order)
    leads = [(1, h, *x) for h in range(LEAD, HG) for x in order]
    leads += [(2, h, *x) for h in range(LEAD) for x in order]
    leads.insert((HG - LEAD) * per + TURN_LAG, None)
    return rounds, order, leads


def width(qt, c):
    return min((qt + 1) * P - c * 512, 512)


def spread(rounds, leads, HG):
    n_rounds = len(rounds)
    cost = []
    for k in range(n_rounds):
        nxt = rounds[(k + AHEAD) % n_rounds][3]
        for h in range(HG):
            pv = rounds[(k + 1) % n_rounds if h == HG - 1 else k][3]
            cost.append(nxt + pv * SHARES[h])
    total = sum(cost)
    need = [0 if x is None else width(x[2], x[3]) for x in leads]
    whole = sum(need)
    out, at, done, spent = [], 0, 0, 0
    for c in cost:
        spent += c
        here = []
        while at < len(leads) and (done + need[at] / 2) * total <= spent * whole:
            here.append(at)
            done += need[at]
            at += 1
        out.append(here)
    out[-1] += list(range(at, len(leads)))
    return out


def build(nc, x, ln_w, ln_b, wq, wk, wv, wo, rw, rb, w1, b1, w2, b2, sw1, sb1, sw2, sb2, out):
    B, S, D = x.shape
    H, _, HD = wq.shape
    HG = 4
    G = H // HG
    T = S // P
    NT = B * T
    N = B * S
    E, _, F = w1.shape
    FC = F // P
    CAP = max(1, N // E)
    VW = HD + 1
    VWIN = (HG - 1) * VW + 32
    VALL = (H - HG) * VW + VWIN
    ROW = 2 * D + 1
    STORES = 3
    STACK = TERMS * HD
    CH = 4
    QSCALE = float(HD) ** -0.5
    assert D == P and H * HD == P and S % 512 == 0

    rounds, order, leads = attention_plan(S, HG)
    NR = len(rounds)
    after = spread(rounds, leads, HG)
    NL = len(leads)
    NU = NL - 1
    PER = len(order)
    PRO = [(0, h, *x) for h in range(HG) for x in order] + \
          [(1, h, *x) for h in range(LEAD) for x in order]
    PRO.insert(HG * PER + TURN_LAG, None)
    diag = [r for r, (qh, kt, q0, n) in enumerate(rounds) if kt * P == q0]

    qd = nc.dram_tensor("q_parts", [B, PARTS, P, S], BF16).ap()
    kd = nc.dram_tensor("k_parts", [B, PARTS, P, S], BF16).ap()
    vd = nc.dram_tensor("v_columns", [B, P, T, VALL], F32).ap()

    def load_group(sp, b, g):
        own = slice(g * HG * HD, (g + 1) * HG * HD)
        for i in range(PARTS):
            at = slice(i * PARTS * HD, (i + 1) * PARTS * HD)
            q_i = qd[b, i, own, :].rearrange("(e h) t -> e (h t)", h=HG)
            sp.dma_start(QS[at, g].rearrange("p h t -> p (h t)"),
                         q_i.unsqueeze(0).broadcast_to([PARTS, HD, HG * S])).then_inc(s_ld[g], 16)
            sp.dma_start(KS[at, g].rearrange("p h t -> p (h t)"),
                         kd[b, :, own, :].rearrange("j (e h) t -> j e (h t)", h=HG)).then_inc(s_ld[g], 16)
        sp.dma_start(VS[:, g], vd[b, :, :, g * HG * VW:g * HG * VW + VWIN]).then_inc(s_ld[g], 16)

    with ExitStack() as ctx:
        def sb(name, shape, dt=F32):
            return ctx.enter_context(nc.sbuf_tensor(name, shape, dt))

        def sem(name):
            return ctx.enter_context(nc.semaphore(name))

        psum = ctx.enter_context(nc.psum_tensor("psum", [P, 8, 512], F32))

        ident = sb("ident", [P, P])
        identb = sb("identb", [P, P], BF16)
        tokens = sb("tokens", [P, B, T, D])
        attn = sb("attn", [P, B, T, D])
        wo_s, rwT, rb_s = sb("wo_s", [P, D]), sb("rwT", [D, E]), sb("rb_s", [P, E])
        s_proj = sem("s_proj")
        empty = sb("empty", [P, ROW])
        attention_bufs = ExitStack()

        def sb_attention(name, shape, dt=F32):
            return attention_bufs.enter_context(nc.sbuf_tensor(name, shape, dt))

        QS = sb_attention("QS", [P, G, HG, S], BF16)
        KS = sb_attention("KS", [P, G, HG, S], BF16)
        VS = sb_attention("VS", [P, G, T, VWIN])
        causal = sb_attention("causal", [P, 512])
        sorted_rows = nc.dram_tensor("sorted_rows", [E * CAP + N, ROW], F32).ap()
        s_empty, s_fill = sem("s_empty"), sem("s_fill")
        s_init = sem("s_init")
        s_ld = [sem(f"s_load{g}") for g in range(G)]
        s_st = [sem("s_store0"), sem("s_store1")]
        s_const = sem("s_const")

        with nc.Block() as block:
            @block.gpsimd
            def _(pool):
                pool.memset(ident[:], 0.0).then_inc(s_const, 1)
                pool.wait_ge(s_const, 1)
                pool.affine_select(out=ident[:], in_=ident[:], compare_op=ALU.not_equal, fill=1.0, base=0,
                                   pattern=[[-1, P]], channel_multiplier=1).then_inc(s_const, 1)
                pool.wait_ge(s_const, 2)
                pool.tensor_copy(identb[:], ident[:]).then_inc(s_const, 1)
                pool.memset(empty[:, 0:2 * D], 0.0).then_inc(s_empty, 1)
                pool.memset(empty[:, 2 * D:].bitcast(U32), N).then_inc(s_empty, 1)

        common = dict(locals())
        prepare(nc, sem, load_group, common)
        attention(nc, sem, load_group, common)
        attention_bufs.close()
        with ExitStack() as late:
            def sb(name, shape, dt=F32):
                return late.enter_context(nc.sbuf_tensor(name, shape, dt))

            rowbuf = sb("rowbuf", [P, B, T, ROW])
            xnT = sb("xnT", [D, B, S])
            logits = sb("logits", [P, E, B, T])
            slot = sb("slot", [P, NT], U32)
            before = sb("before", [P, P], BF16)
            ones = sb("ones", [P, P], BF16)
            rank = sb("rank", [P, E, NT])
            base = sb("base", [P, E, NT])
            fresh = sb("fresh", [P, E, NT])
            own_row = sb("own_row", [P, NT])
            sw1_s, sw2_s = sb("sw1_s", [D, F]), sb("sw2_s", [P, FC, D])
            sb1_s, sb2_s = sb("sb1_s", [P, FC]), sb("sb2_s", [P, D])
            w1_s, w2_s = sb("w1_s", [D, BUFS, F]), sb("w2_s", [P, BUFS, FC, D])
            b1_s, b2_s = sb("b1_s", [P, E, FC]), sb("b2_s", [P, E, D])
            s_tables = sem("s_tables")
            s_shared = sem("s_shared")
            s_ew = [sem(f"s_ew{v}") for v in range(BUFS)]

            def load_shared(eng):
                for dst, src in ((sw1_s[:], sw1), (sw2_s[:], sw2.rearrange("(c p) d -> p c d", p=P)),
                                 (sb2_s[:], sb2.partition_broadcast(P)), (b2_s[:], b2.partition_broadcast(P))):
                    eng.dma_start(dst, src).then_inc(s_shared, 16)
                for dst, src in ((sb1_s[:], sb1.rearrange("(c p) -> p c", p=P)), (b1_s[:], b1.rearrange("e (c p) -> p e c", p=P))):
                    eng.dma_start(dst, src, allow_slow_non_contiguous=True).then_inc(s_shared, 16)

            def load_weights(eng, e, v):
                eng.dma_start(w1_s[:, v], w1[e]).then_inc(s_ew[v], 16)
                eng.dma_start(w2_s[:, v], w2[e].rearrange("(c p) d -> p c d", p=P)).then_inc(s_ew[v], 16)

            project(nc, sem, common | locals())
            mixture(nc, sem, common | locals())


def wait_apart(eng, sem, value, passed):
    eng.wait_ge(sem, value)
    eng.sem_inc(passed, 1)


def prepare(nc, sem, load_group, L):
    (x, ln_w, ln_b, wq, wk, wv, tokens, ident, psum, qd, kd, vd, QS, KS, causal, s_init, s_st, STORES) = (
        L[n] for n in "x ln_w ln_b wq wk wv tokens ident psum qd kd vd QS KS causal s_init s_st STORES".split())
    B, S, D, H, HD, HG, G, T, CH, VW, VWIN, VALL, QSCALE = (
        L[n] for n in "B S D H HD HG G T CH VW VWIN VALL QSCALE".split())
    W = CH * P
    CHAIN = 7
    assert T == 2 * CH
    with ExitStack() as ctx:
        def sb(name, shape, dt=F32):
            return ctx.enter_context(nc.sbuf_tensor(name, shape, dt))

        parts = sb("parts", [P, 2, 2, PARTS, W], BF16)
        vwin = sb("vwin", [P, 2, CH, VALL])
        wq_s, wk_s, wv_s = sb("wq_s", [D, P]), sb("wk_s", [D, P]), sb("wv_s", [D, P])
        wq_r, wk_r = sb("wq_r", [D, H, HD]), sb("wk_r", [D, H, HD])
        gain, shift = sb("gain", [D, 1]), sb("shift", [D, 1])
        stat = sb("stat", [P, T, 6])
        mv = sb("mv", [P, T, 2])
        var = sb("var", [P, 2, T])
        root = sb("root", [P, 2, T])
        inv = sb("inv", [P, 2, T])
        err = sb("err", [P, 2, T])
        scale = sb("scale", [P, 2, T])
        offset = sb("offset", [P, 2, T])
        scale1 = sb("scale1", [P, T])
        y = sb("y", [P, T, D])
        yT = sb("yT", [D, 2, W])
        full = sb("full", [P, 2, 2, W])
        rest = sb("rest", [P, 2, 2, W])

        s_x = [sem(f"s_x{b}") for b in range(B)]
        s_w = sem("s_w")
        s_passed, s_passed_pool = sem("s_passed_prepare"), sem("s_passed_prepare_pool")
        s_wp = sem("s_wp")
        s_vinit = sem("s_vinit")
        s_ln = sem("s_ln")
        s_var, s_sqrt = sem("s_var"), sem("s_sqrt")
        s_scale = sem("s_scale")
        s_scale1 = sem("s_scale1")
        s_y = [sem("s_y0"), sem("s_y1")]
        s_scaled = sem("s_scaled")
        s_sum = sem("s_sum")
        s_yt = sem("s_yt")
        s_yT = sem("s_yT")
        s_prod = [sem("s_q"), sem("s_k")]
        s_v = sem("s_v")
        s_part1 = [sem("s_q_part1"), sem("s_k_part1")]
        s_rest = [sem("s_q_rest"), sem("s_k_rest")]
        s_parts = [sem("s_q_parts"), sem("s_k_parts")]
        s_vw = sem("s_vw")

        with nc.Block() as block:
            @block.sync
            def _(sp):
                def store(b):
                    for u in range(2):
                        for a, dst in ((0, qd), (1, kd)):
                            sp.wait_ge(s_parts[a], 2 * b + u + 1)
                            sp.dma_start(dst[b, :, :, u * W:(u + 1) * W].rearrange("i p t -> p i t"),
                                         parts[:, u, a]).then_inc(s_st[u], 16)
                        sp.wait_ge(s_vw, 2 * b + u + 1)
                        sp.dma_start(vd[b, :, u * CH:(u + 1) * CH, :], vwin[:, u]).then_inc(s_st[u], 16)

                for b in range(B):
                    sp.dma_start(tokens[:, b], x[b].rearrange("(t p) d -> p t d", p=P)).then_inc(s_x[b], 16)
                for b in range(B):
                    store(b)
                    if b == B - 2:
                        sp.wait_ge(s_init, 4)
                        for u in range(2):
                            sp.wait_ge(s_st[u], 16 * STORES)
                        load_group(sp, 0, 0)
            @block.gpsimd
            def _(pool):
                pool.memset(vwin[:, :, :, H * VW:], 0.0).then_inc(s_vinit, 1)
                for u in range(2):
                    pool.memset(vwin[:, u, :, 0:H * VW].rearrange("p t (h v) -> p t h v", v=VW)[:, :, :, HD:], 1.0).then_inc(s_vinit, 1)
                pool.wait_ge(s_vinit, 3)
                pool.memset(QS[64:P].rearrange("p g h t -> p (g h t)").bitcast(U32), 0).then_inc(s_init, 1)
                pool.memset(KS[64:P].rearrange("p g h t -> p (g h t)").bitcast(U32), TWO_ONES).then_inc(s_init, 1)
                pool.wait_ge(s_init, 2)
                pool.memset(causal[:], 0.0).then_inc(s_init, 1)
                pool.wait_ge(s_init, 3)
                pool.affine_select(out=causal[:, 512 - P:], in_=causal[:, 512 - P:], compare_op=ALU.is_ge, fill=MASKED,
                                   base=0, pattern=[[-1, P]], channel_multiplier=1).then_inc(s_init, 1)

                def add(b):
                    x_b = tokens[:, b, 0:CH]
                    pool.wait_ge(s_y[0], b + 1)
                    wait_apart(pool, s_scale1, b + 1, s_passed_pool)
                    pool.tensor_tensor(x_b, x_b, scale1[:, 0:CH].unsqueeze(2).broadcast_to([P, CH, D]), ALU.mult).then_inc(s_scaled, 1)
                    wait_apart(pool, s_scaled, b + 1, s_passed_pool)
                    pool.tensor_tensor(x_b, x_b, offset[:, 0, 0:CH].unsqueeze(2).broadcast_to([P, CH, D]), ALU.add).then_inc(s_sum, 1)

                def split_k(b, u):
                    f, r, p = full[:, u, 1], rest[:, u, 1], parts[:, u, 1]
                    pool.wait_ge(s_part1[1], 2 * b + u + 1)
                    pool.tensor_tensor(p[:, 1], f, p[:, 0], ALU.subtract)
                    pool.tensor_tensor(r, f, p[:, 0], ALU.subtract).then_inc(s_rest[1], 1)
                    pool.wait_ge(s_rest[1], 2 * b + u + 1)
                    pool.tensor_tensor(p[:, 2], r, p[:, 1], ALU.subtract).then_inc(s_parts[1], 1)

                add(0)
                with pool.Fori(0, B - 1) as b:
                    split_k(b, 0)
                    add(b + 1)
                    split_k(b, 1)
                for u in range(2):
                    split_k(B - 1, u)

            @block.vector
            def _(dve):
                def statistics(b):
                    at = CHAIN * b
                    for t in range(T):
                        last = dve.bn_stats(stat[:, t], tokens[:, b, t])
                    last.then_inc(s_ln, 1)
                    wait_apart(dve, s_ln, at + 1, s_passed)
                    for t in range(T):
                        last = dve.bn_aggr(mv[:, t], stat[:, t:t + 1])
                    last.then_inc(s_ln, 1)
                    dve.wait_ge(s_ln, at + 2)
                    dve.tensor_scalar(var[:, 0], mv[:, :, 1], EPS, None, ALU.add)
                    dve.tensor_scalar(var[:, 1], mv[:, :, 1], 1.0 + EPS, EPS * EPS, ALU.mult, ALU.add).then_inc(s_var, 1)

                def scales(b):
                    at = CHAIN * b
                    dve.wait_ge(s_sqrt, b + 1)
                    dve.reciprocal(inv[:], root[:]).then_inc(s_ln, 1)
                    dve.wait_ge(s_ln, at + 3)
                    dve.tensor_tensor(err[:], inv[:], inv[:], ALU.mult).then_inc(s_ln, 1)
                    dve.wait_ge(s_ln, at + 4)
                    dve.tensor_tensor(err[:], err[:], var[:], ALU.mult).then_inc(s_ln, 1)
                    dve.wait_ge(s_ln, at + 5)
                    dve.tensor_scalar(err[:], err[:], -0.5, 1.5, ALU.mult, ALU.add).then_inc(s_ln, 1)
                    dve.wait_ge(s_ln, at + 6)
                    if not isinstance(b, int) or b > 0:
                        dve.wait_ge(s_sum, b)
                    dve.tensor_tensor(scale[:], err[:], inv[:], ALU.mult).then_inc(s_ln, 1)
                    dve.wait_ge(s_ln, at + 7)
                    dve.scalar_tensor_tensor(out=offset[:], in0=mv[:, :, 0].unsqueeze(1).broadcast_to([P, 2, T]), scalar=-1.0,
                                             in1=scale[:], op0=ALU.mult, op1=ALU.mult).then_inc(s_scale, 1)
                    dve.tensor_scalar(scale1[:], scale[:, 0], 1.0, None, ALU.add).then_inc(s_scale1, 1)

                def normalise(b):
                    wait_apart(dve, s_scale, b + 1, s_passed)
                    if not isinstance(b, int) or b > 0:
                        wait_apart(dve, s_yt, 2 * b, s_passed)
                    for t in range(CH, T):
                        last = dve.tensor_scalar(y[:, t], tokens[:, b, t], scale[:, 1, t:t + 1], offset[:, 1, t:t + 1],
                                                 ALU.mult, ALU.add)
                    last.then_inc(s_y[1], 1)
                    wait_apart(dve, s_scale1, b + 1, s_passed)
                    for t in range(CH, T):
                        dve.tensor_scalar(tokens[:, b, t], tokens[:, b, t], scale1[:, t:t + 1], offset[:, 0, t:t + 1],
                                          ALU.mult, ALU.add)

                def split_q(b, u):
                    f, r, p = full[:, u, 0], rest[:, u, 0], parts[:, u, 0]
                    c = 2 * (2 * b + u)
                    dve.wait_ge(s_part1[0], 2 * b + u + 1)
                    dve.tensor_tensor(r, f, p[:, 0], ALU.subtract).then_inc(s_rest[0], 1)
                    dve.wait_ge(s_rest[0], c + 1)
                    dve.tensor_copy(p[:, 1], r).then_inc(s_rest[0], 1)
                    dve.wait_ge(s_rest[0], c + 2)
                    dve.tensor_tensor(p[:, 2], r, p[:, 1], ALU.subtract).then_inc(s_parts[0], 1)

                dve.wait_ge(s_x[0], 16)
                statistics(0)
                scales(0)
                normalise(0)
                dve.wait_ge(s_w, 80)
                for src, dst in ((wq_r, wq_s), (wk_r, wk_s)):
                    dve.tensor_copy(dst[:].rearrange("d (g e h) -> d g e h", g=G, e=HD),
                                    src[:].rearrange("d (g h) e -> d g e h", g=G)).then_inc(s_wp, 1)
                for b in range(1, B):
                    dve.wait_ge(s_x[b], 16)
                with dve.Fori(0, B - 1) as b:
                    statistics(b + 1)
                    scales(b + 1)
                    split_q(b, 0)
                    normalise(b + 1)
                    split_q(b, 1)
                for u in range(2):
                    split_q(B - 1, u)

            @block.tensor
            def _(pe):
                def products(b):
                    later = not isinstance(b, int)
                    if later:
                        pe.wait_ge(s_yT, 2 * b)
                    for u in range(2):
                        pe.wait_ge(s_y[u], b + 1)
                        for t in range(CH):
                            last = pe.transpose(psum[:, u, t * P:(t + 1) * P], y[:, u * CH + t], ident[:])
                        last.then_inc(s_yt, 1)
                    for u in range(2):
                        pe.wait_ge(s_yT, 2 * b + u + 1)
                        for a, w in enumerate((wq_s, wk_s)):
                            if later:
                                pe.wait_ge(s_part1[a], 2 * b + u - 1)
                            pe.matmul(psum[:, 2 + 2 * u + a], w[:], yT[:, u], start=True, stop=True).then_inc(s_prod[a], 1)
                        if later:
                            pe.wait_ge(s_vw, 2 * b + u - 1)
                        for t in range(CH):
                            last = pe.matmul(psum[:, 6 + u, t * P:(t + 1) * P], yT[:, u, t * P:(t + 1) * P], wv_s[:],
                                             start=True, stop=True)
                        last.then_inc(s_v, 1)

                pe.wait_ge(s_wp, 2)
                products(0)
                with pe.Fori(1, B) as b:
                    products(b)

            @block.scalar
            def _(act):
                def roots(b):
                    act.wait_ge(s_var, b + 1)
                    act.activation(root[:], var[:], ACT.Sqrt).then_inc(s_sqrt, 1)

                def normalise(b):
                    act.wait_ge(s_scale, b + 1)
                    if not isinstance(b, int) or b > 0:
                        act.wait_ge(s_yt, 2 * b)
                    for t in range(CH):
                        last = act.activation(y[:, t], tokens[:, b, t], ACT.Identity, bias=offset[:, 1, t:t + 1],
                                              scale=scale[:, 1, t:t + 1])
                    last.then_inc(s_y[0], 1)

                def gains(b):
                    for u in range(2):
                        act.wait_ge(s_yt, 2 * b + u + 1)
                        act.activation(yT[:, u], psum[:, u], ACT.Identity, bias=shift[:], scale=gain[:]).then_inc(s_yT, 1)

                def copies(b, u):
                    if not isinstance(b, int) or b > 0:
                        act.wait_ge(s_st[u], 16 * STORES * b)
                    for a in range(2):
                        act.wait_ge(s_prod[a], 2 * b + u + 1)
                        by = QSCALE if a == 0 else 1.0
                        act.activation(full[:, u, a], psum[:, 2 + 2 * u + a], ACT.Copy, scale=by)
                        act.activation(parts[:, u, a, 0], psum[:, 2 + 2 * u + a], ACT.Copy, scale=by).then_inc(s_part1[a], 1)
                    act.wait_ge(s_v, 2 * b + u + 1)
                    act.activation(vwin[:, u, :, 0:H * VW].rearrange("p t (h v) -> p t h v", v=VW)[:, :, :, 0:HD],
                                   psum[:, 6 + u].rearrange("p (t h e) -> p t h e", t=CH, h=H), ACT.Copy).then_inc(s_vw, 1)

                act.dma_start(wq_r[:], wq.rearrange("h d e -> d h e")).then_inc(s_w, 16)
                act.dma_start(wk_r[:], wk.rearrange("h d e -> d h e")).then_inc(s_w, 16)
                act.dma_start(wv_s[:].rearrange("d (h e) -> d h e", h=H), wv.rearrange("h d e -> d h e")).then_inc(s_w, 16)
                act.dma_start(gain[:], ln_w.rearrange("(d o) -> d o", o=1)).then_inc(s_w, 16)
                act.dma_start(shift[:], ln_b.rearrange("(d o) -> d o", o=1)).then_inc(s_w, 16)
                roots(0)
                normalise(0)
                act.wait_ge(s_w, 80)
                act.wait_ge(s_vinit, 3)

                def step(b):
                    gains(b)
                    roots(b + 1)
                    copies(b, 0)
                    normalise(b + 1)
                    copies(b, 1)

                step(0)
                with act.Fori(1, B - 1) as b:
                    step(b)
                gains(B - 1)
                for u in range(2):
                    copies(B - 1, u)


def attention(nc, sem, load, L):
    (identb, ident, psum, QS, KS, VS, causal, attn, s_init, s_ld, empty, sorted_rows, s_empty, s_fill) = (
        L[n] for n in "identb ident psum QS KS VS causal attn s_init s_ld empty sorted_rows s_empty s_fill".split())
    E, CAP, ROW, wo, rw, rb, wo_s, rwT, rb_s, s_proj, s_st, STORES = (
        L[n] for n in "E CAP ROW wo rw rb wo_s rwT rb_s s_proj s_st STORES".split())
    B, S, D, H, HD, HG, G, T, VW, VWIN, STACK = (L[n] for n in "B S D H HD HG G T VW VWIN STACK".split())
    rounds, leads, after, NR, NL, NU, PRO, diag, PER = (
        L[n] for n in "rounds leads after NR NL NU PRO diag PER".split())
    STEPS = B * G
    PRO_UNITS = len(PRO) - 1
    NC = NR * HG
    HQ = 512
    TURN = leads.index(None)
    whole = T // 2
    halves = [r[0] for r in rounds]
    FIRST_OUT = halves.index(1) + 1
    SECOND_OUT = 1
    LATE = (HG - LEAD) * PER

    def row_buf(g, n):
        return (g * NL + n) % ROWS

    def pro_buf(n):
        return (G * NL - len(PRO) + n) % ROWS

    def row_user(b, g, n):
        e = g * NL + n - ROWS
        if e < 0:
            back = next(k for k in range(ROWS) if (G * NL - 1 - k) % ROWS == g * NL + n)
            return s_max, PRO_UNITS + b * G * NU - back
        gg, nn = divmod(e, NL)
        i = b * G + gg
        if nn == TURN:
            return s_mrow, i + 2
        return s_max, PRO_UNITS + i * NU + nn + (nn < TURN)
    mturn_at = [n for n, a in enumerate(after) if leads.index(None) in a][0]
    with ExitStack() as ctx:
        def sb(name, shape, dt=F32):
            return ctx.enter_context(nc.sbuf_tensor(name, shape, dt))

        probs = sb("probs", [P, 4, HG, HQ])
        rowmax = sb("rowmax", [P, 2, T, HG])
        left = sb("left", [P, 2, 2, T, HG])
        firstmax = sb("firstmax", [P, 2, T // 2, HG])
        negm = sb("negm", [P, 2, T, PARTS, HG], BF16)
        mrow = sb("mrow", [PARTS * HG, 2, S], BF16)
        osum = sb("osum", [P, 2, HQ])
        rden = sb("rden", [P, 2, HQ // P, HG])

        rows = [psum[:, i] for i in range(ROWS)]
        cols = [psum[:, ROWS + i] for i in range(COLS)]
        outs = [psum[:, 6], psum[:, 7]]

        s_passed_dve = sem("s_passed_dve")
        s_passed_pool = sem("s_passed_pool")
        s_ml = [sem(f"s_mload{g}") for g in range(G)]
        s_rows = sem("s_rows")
        s_max = sem("s_max")
        s_pool = sem("s_pool")
        s_whole = sem("s_whole")
        s_negm = sem("s_negm")
        s_mturn = sem("s_mturn")
        s_mrow = sem("s_mrow")
        s_cols = sem("s_cols")
        s_exp = sem("s_exp")
        s_mask = sem("s_mask")
        s_pv = sem("s_pv")
        s_oevac = [sem("s_oevac0"), sem("s_oevac1")]
        s_oturn = [sem("s_oturn0"), sem("s_oturn1")]
        s_rden = sem("s_rden")
        s_norm = [sem("s_norm0"), sem("s_norm1")]
        NLD = 2 * PARTS + 1

        def plus(b, g):
            return b + g // G, g % G

        with nc.Block() as block:
            @block.sync
            def _(sp):
                def load_maxima(b, g):
                    sp.wait_ge(s_mrow, G * b + g + 1)
                    for i in range(PARTS):
                        sp.dma_start(QS[STACK + i:STACK + i + 1, g], mrow[i * HG:(i + 1) * HG, g % 2]).then_inc(s_ml[g], 16)

                def step(b, g, left_groups):
                    if left_groups > 3:
                        sp.wait_ge(s_pv, (b * G + g) * NR + 1)
                        load(sp, *plus(b, g + 3))
                    if left_groups > 1:
                        load_maxima(*plus(b, g + 1))

                for g in range(1, 3):
                    load(sp, 0, g)
                for g in range(G):
                    sp.sem_inc(s_ml[g], 16)
                for u in range(2):
                    sp.wait_ge(s_st[u], 16 * STORES * B)
                load_maxima(0, 0)
                with sp.Fori(0, B - 1) as b:
                    for g in range(G):
                        step(b, g, G)
                for g in range(G):
                    step(B - 1, g, G - g)
                sp.dma_start(wo_s[:], wo).then_inc(s_proj, 16)
                sp.dma_start(rwT[:], rw.rearrange("e d -> d e"), allow_slow_non_contiguous=True).then_inc(s_proj, 16)
                sp.dma_start(rb_s[:], rb.partition_broadcast(P)).then_inc(s_proj, 16)
                sp.wait_ge(s_empty, 2)
                sp.dma_start(sorted_rows[0:E * CAP].rearrange("(t p) c -> p t c", p=P),
                             empty[:].unsqueeze(1).broadcast_to([P, E * CAP // P, ROW])).then_inc(s_fill, 16)

            @block.gpsimd
            def _(pool):
                def split_maxima(b, g):
                    i, w = G * b + g, g % 2
                    m, l, n = rowmax[:, w], left[:, w], negm[:, w]
                    wait_apart(pool, s_whole, i + 1, s_passed_pool)
                    if not isinstance(i, int) or i >= 2:
                        wait_apart(pool, s_mturn, i, s_passed_pool)
                    pool.tensor_scalar(n[:, :, 0], m, -1.0, None, ALU.mult).then_inc(s_pool, 1)
                    wait_apart(pool, s_pool, 4 * i + 1, s_passed_pool)
                    pool.tensor_tensor(l[:, 0], m, n[:, :, 0], ALU.add).then_inc(s_pool, 1)
                    wait_apart(pool, s_pool, 4 * i + 2, s_passed_pool)
                    pool.tensor_scalar(n[:, :, 1], l[:, 0], -1.0, None, ALU.mult).then_inc(s_pool, 1)
                    wait_apart(pool, s_pool, 4 * i + 3, s_passed_pool)
                    pool.tensor_tensor(l[:, 1], l[:, 0], n[:, :, 1], ALU.add).then_inc(s_pool, 1)
                    wait_apart(pool, s_pool, 4 * i + 4, s_passed_pool)
                    pool.tensor_scalar(n[:, :, 2], l[:, 1], -1.0, None, ALU.mult).then_inc(s_negm, 1)

                def step(b, g, left_groups):
                    i = b * G + g
                    masks = [r for r in range(AHEAD, NR)] + [NR + r for r in range(AHEAD)]
                    for n, r in enumerate(masks):
                        if r % NR in diag and (r < NR or left_groups > 1):
                            mask(i + r // NR, r % NR)
                        if n == 3 and left_groups > 1:
                            split_maxima(*plus(b, g + 1))

                def mask(i, r):
                    wait_apart(pool, s_exp, (i * NR + r + 1) * HG, s_passed_pool)
                    tri = probs[:, r % 4, :, 0:P]
                    pool.affine_select(out=tri, in_=tri, compare_op=ALU.is_ge, fill=0.0, base=0,
                                       pattern=[[0, HG], [1, P]], channel_multiplier=-1).then_inc(s_mask, 1)

                split_maxima(0, 0)
                for r in range(AHEAD):
                    if r in diag:
                        mask(0, r)
                with pool.Fori(0, B - 1) as b:
                    for g in range(G):
                        step(b, g, G)
                for g in range(G):
                    step(B - 1, g, G - g)

            @block.tensor
            def _(pe):
                def lead(buf, b, g, h, qt, c, first, free):
                    if first:
                        pe.wait_ge(s_ld[g], 16 * NLD * (b + 1))
                    if free is not None:
                        pe.wait_ge(*free)
                    w = width(qt, c)
                    pe.matmul(rows[buf][:, 0:w], QS[0:STACK, g, h, qt * P:(qt + 1) * P],
                              KS[0:STACK, g, h, c * 512:c * 512 + w], start=True, stop=True).then_inc(s_rows, 1)

                def turn_maxima(buf, b, g, free):
                    pe.wait_ge(*free)
                    pe.wait_ge(s_negm, G * b + g + 1)
                    dst = rows[buf].bitcast(BF16)
                    for t in range(T):
                        last = pe.transpose(dst[0:PARTS * HG, t * P:(t + 1) * P],
                                            negm[:, g % 2, t].rearrange("p i h -> p (i h)"), identb[:])
                    last.then_inc(s_mturn, 1)

                def col(b, g, r, h):
                    i = b * G + g
                    qh, kt, q0, n = rounds[r]
                    if r == 0 and h == 0:
                        pe.wait_ge(s_ml[g], 16 * (PARTS * (b + 1) + 1))
                    c = r * HG + h
                    if not isinstance(i, int) or i * NC + c >= COLS:
                        pe.wait_ge(s_exp, i * NC + c - COLS + 1)
                    pe.matmul(cols[c % COLS][:, 0:n], KS[:, g, h, kt * P:(kt + 1) * P], QS[:, g, h, q0:q0 + n],
                              start=True, stop=True).then_inc(s_cols, 1)

                def values(b, g, r):
                    i = b * G + g
                    qh, kt, q0, n = rounds[r]
                    if kt == 0:
                        pe.wait_ge(s_norm[qh], i + 1)
                    if r in diag:
                        pe.wait_ge(s_mask, i * len(diag) + diag.index(r) + 1)
                    else:
                        pe.wait_ge(s_exp, (i * NR + r + 1) * HG)
                    last_kt = (qh + 1) * HQ // P - 1
                    for h in range(HG):
                        last = pe.matmul(outs[qh][32 * h:32 * h + 32, q0 - qh * HQ:HQ],
                                         VS[:, g, kt, h * VW:h * VW + 32], probs[:, r % 4, h, 0:n],
                                         start=(kt == 0), stop=(kt == last_kt), skip_group_check=True)
                    last.then_inc(s_pv, 1)

                def turn_out(b, g, qh):
                    pe.wait_ge(s_oevac[qh], b * G + g + 1)
                    for t in range(HQ // P):
                        last = pe.transpose(outs[qh][:, t * P:(t + 1) * P], osum[:, qh, t * P:(t + 1) * P], ident[:])
                    last.then_inc(s_oturn[qh], 1)

                def step(b, g, left_groups, before):
                    i = b * G + g
                    for k in range(NR):
                        values(b, g, k)
                        for h in range(HG):
                            r = k + AHEAD
                            if r < NR:
                                col(b, g, r, h)
                            elif left_groups > 1:
                                col(*plus(b, g + 1), r - NR, h)
                            for n in after[k * HG + h]:
                                x = leads[n]
                                ahead = 1 if x is None else x[0]
                                if left_groups <= ahead:
                                    continue
                                buf = row_buf(g, n)
                                if x is None:
                                    free = row_user(b, g, n) if left_groups > 2 else (s_max, PRO_UNITS + i * NU + LATE)
                                    turn_maxima(buf, *plus(b, g + 1), free)
                                else:
                                    bb, gg = plus(b, g + x[0])
                                    lead(buf, bb, gg, *x[1:], n == LATE, row_user(b, g, n))
                        if k == SECOND_OUT and before is not None:
                            turn_out(*before, 1)
                        if k == FIRST_OUT:
                            turn_out(b, g, 0)

                for s in (s_pv, s_mturn):
                    pe.sem_inc(s, 1)
                pe.wait_ge(s_init, 4)
                turn = PRO.index(None)
                for n, x in enumerate(PRO):
                    free = None
                    if n >= ROWS:
                        before = n - ROWS
                        free = (s_mrow, 1) if before == turn else (s_max, before + (before < turn))
                    if x is None:
                        turn_maxima(pro_buf(n), 0, 0, free)
                    else:
                        lead(pro_buf(n), 0, *x, n % (HG * PER) == 0, free)
                    c, odd = divmod(n - (len(PRO) - 2 * AHEAD * HG), 2)
                    if c >= 0 and odd:
                        col(0, 0, c // HG, c % HG)
                step(0, 0, G, None)
                with pe.Fori(0, B - 1) as b:
                    for g in range(G):
                        step(*plus(b, g + 1), G, (b, g))
                for g in range(1, G):
                    step(B - 1, g, G - g, (B - 1, g - 1))
                turn_out(B - 1, G - 1, 1)

            @block.scalar
            def _(act):
                def exps(b, g, r, turn=None):
                    i = b * G + g
                    n = rounds[r][3]
                    R = i * NR + r
                    if not isinstance(i, int) or R >= 4:
                        act.wait_ge(s_pv, i * NR + max(r - 3, 0) + 1 if r >= AHEAD else R - 2)
                    for h in range(HG):
                        act.wait_ge(s_cols, R * HG + h + 1)
                        act.activation(probs[:, r % 4, h, 0:n], cols[(r * HG + h) % COLS][:, 0:n], ACT.Exp).then_inc(s_exp, 1)
                        if turn is not None and turn[0] == h:
                            maxima(*turn[1:])

                def evac(b, g, qh):
                    i = b * G + g
                    last = [r for r in range(NR) if rounds[r][0] == qh][-1]
                    act.wait_ge(s_pv, i * NR + last + 2)
                    act.activation(osum[:, qh], outs[qh], ACT.Copy).then_inc(s_oevac[qh], 1)

                def maxima(b, g, buf):
                    act.wait_ge(s_mturn, b * G + g + 2)
                    if g >= 2:
                        act.wait_ge(s_ml[g - 2], 16 * (PARTS * (b + 1) + 1))
                    else:
                        act.wait_ge(s_ml[g + 2], 16 * (PARTS * b + 1))
                    act.activation(mrow[:, g % 2], rows[buf].bitcast(BF16)[0:PARTS * HG], ACT.Copy).then_inc(s_mrow, 1)

                def step(b, g, left_groups, before):
                    for k in range(NR):
                        r = k + AHEAD
                        turn = None
                        if k == mturn_at // HG and left_groups > 1:
                            turn = (mturn_at % HG, *plus(b, g + 1), row_buf(g, TURN))
                        if r < NR:
                            exps(b, g, r, turn)
                        elif left_groups > 1:
                            exps(*plus(b, g + 1), r - NR, turn)
                        if k == SECOND_OUT - 1 and before is not None:
                            evac(*before, 1)
                        if k == FIRST_OUT - 1:
                            evac(b, g, 0)

                for u in range(2):
                    act.wait_ge(s_st[u], 16 * STORES * B)
                maxima(0, 0, pro_buf(PRO.index(None)))
                for r in range(AHEAD):
                    exps(0, 0, r)
                step(0, 0, G, None)
                with act.Fori(0, B - 1) as b:
                    for g in range(G):
                        step(*plus(b, g + 1), G, (b, g))
                for g in range(1, G):
                    step(B - 1, g, G - g, (B - 1, g - 1))
                evac(B - 1, G - 1, 1)

            @block.vector
            def _(dve):
                def maxima(buf, m, w, h, qt, c):
                    n = width(qt, c)
                    tile = rows[buf][:, 0:n]
                    if c * 512 + n == (qt + 1) * P:
                        wait_apart(dve, s_rows, m + 1, s_passed_dve)
                        dve.wait_ge(s_init, 4)
                        dve.tensor_tensor_reduce(tile, tile, causal[:, 512 - n:], 1.0, MASKED, ALU.add, ALU.max,
                                                 rowmax[:, w, qt, h:h + 1]).then_inc(s_max, 1)
                    else:
                        dve.wait_ge(s_rows, m + 1)
                        dve.reduce_max(firstmax[:, w, qt - whole, h:h + 1], tile, AX.X).then_inc(s_max, 1)

                def join(w, count):
                    dve.wait_ge(s_max, count)
                    m = rowmax[:, w, whole:]
                    dve.tensor_tensor(m, m, firstmax[:, w], ALU.max).then_inc(s_whole, 1)

                def norm(b, g, qh):
                    i = b * G + g
                    dve.wait_ge(s_oturn[qh], i + 1)
                    o = outs[qh].rearrange("p (t h v) -> p t h v", t=HQ // P, h=HG)
                    dve.reciprocal(rden[:, qh], o[:, :, :, HD]).then_inc(s_rden, 1)
                    dve.wait_ge(s_rden, 2 * i + qh + 1)
                    nt = HQ // P
                    dst = attn[:, b, qh * nt:(qh + 1) * nt, g * HG * HD:(g + 1) * HG * HD].rearrange("p t (h e) -> p t h e", h=HG)
                    dve.tensor_tensor(dst, o[:, :, :, 0:HD], rden[:, qh].unsqueeze(3).broadcast_to([P, nt, HG, HD]),
                                      ALU.mult).then_inc(s_norm[qh], 1)

                def step(b, g, left_groups, before):
                    i = b * G + g
                    units = PRO_UNITS + i * NU
                    for k in range(NR):
                        for h in range(HG):
                            for n in after[k * HG + h]:
                                x = leads[n]
                                if left_groups == 2 and n == LATE + 1:
                                    join((g + 1) % 2, units + LATE)
                                if x is None or left_groups <= x[0]:
                                    continue
                                done = sum(1 for e in leads[:n] if e is not None)
                                gg = (g + x[0]) % G
                                maxima(row_buf(g, n), units + done, gg % 2, *x[1:])
                                if n == LATE + 1:
                                    join((g + 1) % 2, units + LATE)
                        if k == SECOND_OUT and before is not None:
                            norm(*before, 1)
                        if k == FIRST_OUT:
                            norm(b, g, 0)

                for qh in range(2):
                    dve.sem_inc(s_norm[qh], 1)
                m = 0
                for n, x in enumerate(PRO):
                    if x is not None:
                        maxima(pro_buf(n), m, x[0] % 2, *x[1:])
                        m += 1
                    if n == HG * PER + 1:
                        join(0, HG * PER)
                step(0, 0, G, None)
                with dve.Fori(0, B - 1) as b:
                    for g in range(G):
                        step(*plus(b, g + 1), G, (b, g))
                for g in range(1, G):
                    step(B - 1, g, G - g, (B - 1, g - 1))
                norm(B - 1, G - 1, 1)


def project(nc, sem, L):
    (attn, tokens, ident, psum, rowbuf, xnT, logits, wo_s, rwT, rb_s, s_proj) = (
        L[n] for n in "attn tokens ident psum rowbuf xnT logits wo_s rwT rb_s s_proj".split())
    (before, ones, rank, base, fresh, own_row, s_tables, load_weights, load_shared) = (
        L[n] for n in "before ones rank base fresh own_row s_tables load_weights load_shared".split())
    B, S, D, T, NT, CH, E, CAP = (L[n] for n in "B S D T NT CH E CAP".split())
    W = CH * P
    CHAIN = 7
    with ExitStack() as ctx:
        def sb(name, shape, dt=F32):
            return ctx.enter_context(nc.sbuf_tensor(name, shape, dt))

        aT = sb("aT", [P, 2, W])
        stat = sb("stat2", [P, T, 6])
        mv = sb("mv2", [P, T, 2])
        small = {n: sb(n + "2", [P, T]) for n in "var root inv err scale offset".split()}
        var, root, inv, err, scale, offset = small.values()

        s_passed = sem("s_passed_project")
        s_at = sem("s_at")
        s_aT = sem("s_aT")
        s_o = sem("s_o")
        s_x1 = sem("s_resid")
        s_ln = sem("s_ln2")
        s_var, s_sqrt, s_scale = sem("s_var2"), sem("s_sqrt2"), sem("s_scale2")
        s_xn = [sem("s_xn0"), sem("s_xn1")]
        s_xt = sem("s_xn_turned")
        s_xT = sem("s_xnT")
        s_lg = sem("s_lg")
        s_lgd = sem("s_lgd")

        with nc.Block() as block:
            @block.sync
            def _(sp):
                load_shared(sp)
                for e in range(BUFS):
                    load_weights(sp, e, e)

            @block.gpsimd
            def _(pool):
                made = [0]

                def table(ins):
                    ins.then_inc(s_tables, 1)
                    made[0] += 1
                    pool.wait_ge(s_tables, made[0])

                table(pool.iota(rowbuf[:, :, :, 2 * D:].bitcast(U32), pattern=[[S, B], [P, T], [1, 1]], base=0,
                                channel_multiplier=1))
                table(pool.memset(before[:], 1.0))
                table(pool.affine_select(out=before[:], in_=before[:], compare_op=ALU.is_gt, fill=0.0, base=0,
                                         pattern=[[1, P]], channel_multiplier=-1))
                table(pool.memset(ones[:], 1.0))
                table(pool.iota(rank[:], pattern=[[-1, E], [0, NT]], base=E, channel_multiplier=0,
                                allow_small_or_imprecise_dtypes=True))
                table(pool.iota(base[:], pattern=[[CAP, E], [0, NT]], base=0, channel_multiplier=0,
                                allow_small_or_imprecise_dtypes=True))
                table(pool.iota(own_row[:], pattern=[[P, NT]], base=E * CAP, channel_multiplier=1,
                                allow_small_or_imprecise_dtypes=True))
                table(pool.memset(fresh[:], 1.0))
                table(pool.memset(fresh[:, :, 0:1], 0.0))

            @block.vector
            def _(dve):
                def x1(b):
                    return rowbuf[:, b, :, D:2 * D]

                def residual(b, u):
                    at = slice(u * CH, (u + 1) * CH)
                    dve.wait_ge(s_o, 2 * b + u + 3)
                    dve.tensor_tensor(x1(b)[:, at], tokens[:, b, at], psum[:, 2 + u].rearrange("p (t d) -> p t d", t=CH),
                                      ALU.add).then_inc(s_x1, 1)

                def statistics(b):
                    at = CHAIN * b
                    wait_apart(dve, s_x1, 2 * b + 4, s_passed)
                    for t in range(T):
                        last = dve.bn_stats(stat[:, t], x1(b)[:, t])
                    last.then_inc(s_ln, 1)
                    wait_apart(dve, s_ln, at + 1, s_passed)
                    for t in range(T):
                        last = dve.bn_aggr(mv[:, t], stat[:, t:t + 1])
                    last.then_inc(s_ln, 1)
                    dve.wait_ge(s_ln, at + 2)
                    dve.tensor_scalar(var[:], mv[:, :, 1], EPS, None, ALU.add).then_inc(s_var, 1)

                def scales(b):
                    at = CHAIN * b
                    dve.wait_ge(s_sqrt, b + 1)
                    dve.reciprocal(inv[:], root[:]).then_inc(s_ln, 1)
                    dve.wait_ge(s_ln, at + 3)
                    dve.tensor_tensor(err[:], inv[:], inv[:], ALU.mult).then_inc(s_ln, 1)
                    dve.wait_ge(s_ln, at + 4)
                    dve.tensor_tensor(err[:], err[:], var[:], ALU.mult).then_inc(s_ln, 1)
                    dve.wait_ge(s_ln, at + 5)
                    dve.tensor_scalar(err[:], err[:], -0.5, 1.5, ALU.mult, ALU.add).then_inc(s_ln, 1)
                    dve.wait_ge(s_ln, at + 6)
                    dve.tensor_tensor(scale[:], err[:], inv[:], ALU.mult).then_inc(s_ln, 1)
                    dve.wait_ge(s_ln, at + 7)
                    dve.scalar_tensor_tensor(out=offset[:], in0=mv[:, :, 0], scalar=-1.0, in1=scale[:],
                                             op0=ALU.mult, op1=ALU.mult).then_inc(s_scale, 1)

                def normalise(b):
                    for t in range(CH, T):
                        last = dve.tensor_scalar(rowbuf[:, b, t, 0:D], x1(b)[:, t], mv[:, t, 0:1], scale[:, t:t + 1],
                                                 ALU.subtract, ALU.mult)
                    last.then_inc(s_xn[1], 1)

                def front(b):
                    for u in range(2):
                        residual(b, u)
                    statistics(b)
                    scales(b)
                    normalise(b)

                def add_bias(b):
                    dve.wait_ge(s_lg, b + 2)
                    dve.tensor_tensor(logits[:, :, b, :].rearrange("p e t -> p t e"),
                                      psum[:, 6, 0:T * E].rearrange("p (t e) -> p t e", t=T),
                                      rb_s[:].unsqueeze(1).broadcast_to([P, T, E]), ALU.add).then_inc(s_lgd, 1)

                dve.sem_inc(s_x1, 2)
                dve.sem_inc(s_lgd, 1)
                dve.wait_ge(s_proj, 48)
                front(0)
                with dve.Fori(0, B - 1) as b:
                    front(b + 1)
                    add_bias(b)
                add_bias(B - 1)

            @block.tensor
            def _(pe):
                def turn_in(b):
                    pe.wait_ge(s_aT, 2 * b + 2)
                    for u in range(2):
                        for t in range(CH):
                            last = pe.transpose(psum[:, u, t * P:(t + 1) * P], attn[:, b, u * CH + t], ident[:])
                        last.then_inc(s_at, 1)

                def out_projection(b):
                    for u in range(2):
                        pe.wait_ge(s_aT, 2 * b + u + 3)
                        pe.wait_ge(s_x1, 2 * b + u + 1)
                        for t in range(CH):
                            last = pe.matmul(psum[:, 2 + u, t * P:(t + 1) * P], aT[:, u, t * P:(t + 1) * P], wo_s[:],
                                             start=True, stop=True)
                        last.then_inc(s_o, 1)

                def turn_out(b):
                    for u in range(2):
                        pe.wait_ge(s_xn[u], b + 1)
                        pe.wait_ge(s_xT, 2 * b + u + 1)
                        for t in range(CH):
                            last = pe.transpose(psum[:, 4 + u, t * P:(t + 1) * P], rowbuf[:, b, u * CH + t, 0:D], ident[:])
                        last.then_inc(s_xt, 1)

                def router(b):
                    pe.wait_ge(s_lgd, b + 1)
                    for u in range(2):
                        pe.wait_ge(s_xT, 2 * b + u + 3)
                        for t in range(CH):
                            last = pe.matmul(psum[:, 6, (u * CH + t) * E:(u * CH + t + 1) * E],
                                             xnT[:, b, (u * CH + t) * P:(u * CH + t + 1) * P], rwT[:], start=True, stop=True)
                    last.then_inc(s_lg, 1)

                for s, n in ((s_at, 2), (s_o, 2), (s_xt, 2), (s_lg, 1)):
                    pe.sem_inc(s, n)
                pe.wait_ge(s_proj, 48)
                for b in range(2):
                    turn_in(b)
                    out_projection(b)
                for b in range(B):
                    if b + 2 < B:
                        turn_in(b + 2)
                    turn_out(b)
                    if b + 2 < B:
                        out_projection(b + 2)
                    router(b)

            @block.scalar
            def _(act):
                def copy_in(b):
                    for u in range(2):
                        act.wait_ge(s_at, 2 * b + u + 3)
                        act.wait_ge(s_o, 2 * b + u + 1)
                        act.activation(aT[:, u], psum[:, u], ACT.Copy).then_inc(s_aT, 1)

                def copy_out(b):
                    for u in range(2):
                        act.wait_ge(s_xt, 2 * b + u + 3)
                        act.activation(xnT[:, b, u * W:(u + 1) * W], psum[:, 4 + u], ACT.Copy).then_inc(s_xT, 1)

                def roots(b):
                    act.wait_ge(s_var, b + 1)
                    act.activation(root[:], var[:], ACT.Sqrt).then_inc(s_sqrt, 1)

                def normalise(b):
                    act.wait_ge(s_scale, b + 1)
                    for t in range(CH):
                        last = act.activation(rowbuf[:, b, t, 0:D], rowbuf[:, b, t, D:2 * D], ACT.Identity, bias=offset[:, t:t + 1],
                                              scale=scale[:, t:t + 1])
                    last.then_inc(s_xn[0], 1)

                for s in (s_aT, s_xT):
                    act.sem_inc(s, 2)
                copy_in(0)
                copy_in(1)
                roots(0)
                normalise(0)
                with act.Fori(0, B - 2) as b:
                    copy_in(b + 2)
                    copy_out(b)
                    roots(b + 1)
                    normalise(b + 1)
                copy_out(B - 2)
                roots(B - 1)
                normalise(B - 1)
                copy_out(B - 1)


def mixture(nc, sem, L):
    (psum, ident, rowbuf, xnT, logits, slot, sorted_rows, s_fill, s_tables, s_shared, s_ew, load_weights, out) = (
        L[n] for n in "psum ident rowbuf xnT logits slot sorted_rows s_fill s_tables s_shared s_ew load_weights out".split())
    (before, ones, rank, base, fresh, own_row, sw1_s, sb1_s, sw2_s, sb2_s, w1_s, b1_s, w2_s, b2_s) = (
        L[n] for n in "before ones rank base fresh own_row sw1_s sb1_s sw2_s sb2_s w1_s b1_s w2_s b2_s".split())
    B, N, S, NT, E, CAP, ROW, D, F, FC, CH = (L[n] for n in "B N S NT E CAP ROW D F FC CH".split())
    W = CH * P
    JOBS = N // W
    CHOSEN = E * NT
    flat = "p e t -> p (e t)"
    assert CAP == W and S == 2 * W and E % BUFS == 0 and BUFS == 4
    with ExitStack() as ctx:
        def sb(name, shape, dt=F32):
            return ctx.enter_context(nc.sbuf_tensor(name, shape, dt))

        bufs = {n: sb(n, [P, E, NT]) for n in "gate pick weigh pos1 pos2 incl one two prod".split()}
        gate, pick, weigh, pos1, pos2, incl, one, two, prod = bufs.values()
        oneb, twob = sb("oneb", [P, E, NT], BF16), sb("twob", [P, E, NT], BF16)
        small = sb("small", [P, 11, NT])
        used = sb("used", [P, E])
        warm = sb("warm", [P, 1])
        xs = sb("xs", [P, BUFS, CH, ROW])
        xsT = sb("xsT", [D, 2, W])
        hid = sb("hid", [P, 2, FC, W])
        res = sb("res", [P, BUFS, CH, D])

        s_passed, s_passed_pool = sem("s_passed_mixture"), sem("s_passed_mixture_pool")
        s_route = sem("s_route")
        s_exp = sem("s_exp_gate")
        s_one, s_cum = sem("s_one"), sem("s_cum")
        s_slot = sem("s_slot")
        s_sent = sem("s_sent")
        s_h = sem("s_h")
        s_g = sem("s_g")
        s_yy = sem("s_yy")
        s_add, s_res = sem("s_add"), sem("s_res")
        s_out = [sem("s_out0"), sem("s_out1")]
        s_xs = [sem(f"s_xs{v}") for v in range(BUFS)]
        s_xt, s_xT = sem("s_xt"), sem("s_xT")
        s_put = [sem(f"s_put{v}") for v in range(BUFS)]

        with nc.Block() as block:
            def rows_of(eng, e, v):
                eng.dma_start(xs[:, v], sorted_rows.rearrange("(k t p) c -> k p t c", t=CH, p=P)[e]).then_inc(s_xs[v], 16)

            @block.sync
            def _(sp):
                for u in range(2):
                    sp.sem_inc(s_out[u], 16)
                with sp.Fori(0, B) as b:
                    for u in range(2):
                        sp.wait_ge(s_res, 2 * b + u + 1)
                        sp.dma_start(out[b].rearrange("(k t p) d -> k p t d", k=2, p=P)[u], res[:, u]).then_inc(s_out[u], 16)
                for u in range(2):
                    sp.wait_ge(s_out[u], 16 * (B + 1))
                for e in range(BUFS, E):
                    v = e % BUFS
                    sp.wait_ge(s_yy, JOBS + e - BUFS + 3)
                    load_weights(sp, e, v)
                    sp.wait_ge(s_put[v], 16 * CH * (e // BUFS))
                    rows_of(sp, e, v)

            @block.gpsimd
            def _(pool):
                pool.wait_ge(s_fill, 16)
                pool.wait_ge(s_slot, 1)
                for t in range(NT):
                    pool.indirect_dma_start(out=sorted_rows, out_offset=bass.IndirectOffsetOnAxis(ap=slot[:, t:t + 1], axis=0),
                                            in_=rowbuf[:].rearrange("p b t c -> p (b t) c")[:, t], in_offset=None).then_inc(s_sent, 16)
                for u in range(2):
                    pool.wait_ge(s_out[u], 16 * (B + 1))
                last_token = pool.to_reg(N - 1)
                with pool.Fori(0, E // BUFS) as k:
                    for v in range(BUFS):
                        for t in range(CH):
                            if t == 0:
                                wait_apart(pool, s_res, JOBS + BUFS * k + v + 1, s_passed_pool)
                            pool.indirect_dma_start(
                                out=out.rearrange("b s d -> (b s) d"),
                                out_offset=bass.IndirectOffsetOnAxis(ap=xs[:, v, t, 2 * D:].bitcast(U32), axis=0),
                                in_=res[:, v, t], in_offset=None, bounds_check=last_token, oob_is_err=False).then_inc(s_put[v], 16)
                for v in range(BUFS):
                    pool.wait_ge(s_put[v], 16 * CH * (E // BUFS))

            @block.tensor
            def _(pe):
                def up(j, u, w, x):
                    for c in range(FC):
                        pe.wait_ge(s_g, FC * j + c + 1)
                        pe.matmul(psum[:, c], w[:, c * P:(c + 1) * P], x, start=True, stop=True).then_inc(s_h, 1)

                def down(j, u, w):
                    pe.wait_ge(s_g, FC * (j + 2))
                    pe.wait_ge(s_add, j + 1)
                    for t in range(CH):
                        for c in range(FC):
                            last = pe.matmul(psum[:, 4 + u, t * P:(t + 1) * P], hid[:, u, c, t * P:(t + 1) * P], w[:, c],
                                             start=(c == 0), stop=(c == FC - 1))
                    last.then_inc(s_yy, 1)

                def count_before(n, chosen):
                    pe.wait_ge(s_one, n + 1)
                    pe.matmul(psum[:, 6 + n, 0:CHOSEN], before[:], chosen[:].rearrange(flat), start=True, stop=True)
                    pe.matmul(psum[:, 6 + n, CHOSEN:2 * CHOSEN], ones[:], chosen[:].rearrange(flat),
                              start=True, stop=True).then_inc(s_cum, 1)

                pe.sem_inc(s_yy, 2)
                pe.wait_ge(s_shared, 96)
                for u in range(2):
                    up(u, u, sw1_s, xnT[:, 0, u * W:(u + 1) * W])
                count_before(0, oneb)
                down(0, 0, sw2_s)
                count_before(1, twob)
                down(1, 1, sw2_s)
                with pe.Fori(1, B) as b:
                    for u in range(2):
                        up(2 * b + u, u, sw1_s, xnT[:, b, u * W:(u + 1) * W])
                    for u in range(2):
                        down(2 * b + u, u, sw2_s)
                with pe.Fori(0, E // BUFS) as k:
                    for v0 in range(0, BUFS, 2):
                        e = BUFS * k + v0
                        for u in range(2):
                            pe.wait_ge(s_xs[v0 + u], 16 * (k + 1))
                            pe.wait_ge(s_xT, e + u + 1)
                            for t in range(CH):
                                last = pe.transpose(psum[:, 6 + u, t * P:(t + 1) * P], xs[:, v0 + u, t, 0:D], ident[:])
                            last.then_inc(s_xt, 1)
                        for u in range(2):
                            pe.wait_ge(s_ew[v0 + u], 32 * (k + 1))
                            pe.wait_ge(s_xT, e + u + 3)
                            up(JOBS + e + u, u, w1_s[:, v0 + u], xsT[:, u])
                        for u in range(2):
                            down(JOBS + e + u, u, w2_s[:, v0 + u])

            @block.scalar
            def _(act):
                def gelu(j, u, bias):
                    for c in range(FC):
                        act.wait_ge(s_h, FC * j + c + 1)
                        if c == 0:
                            act.wait_ge(s_yy, j + 1)
                        act.activation(hid[:, u, c], psum[:, c], ACT.Gelu, bias=bias(c)).then_inc(s_g, 1)

                act.sem_inc(s_g, FC)
                act.sem_inc(s_xT, 2)
                act.wait_ge(s_shared, 96)
                act.activation(warm[:], sb2_s[:, 0:1], ACT.Exp)
                act.wait_ge(s_route, 2)
                act.activation(pick[:], gate[:], ACT.Exp).then_inc(s_exp, 1)
                with act.Fori(0, B) as b:
                    for u in range(2):
                        gelu(2 * b + u, u, lambda c: sb1_s[:, c:c + 1])
                act.wait_ge(s_sent, 16 * NT)
                for v in range(BUFS):
                    rows_of(act, v, v)
                with act.Fori(0, E // BUFS) as k:
                    for v0 in range(0, BUFS, 2):
                        e = BUFS * k + v0
                        for u in range(2):
                            act.wait_ge(s_xt, e + u + 1)
                            act.wait_ge(s_h, FC * (JOBS + e + u - 1))
                            act.activation(xsT[:, u], psum[:, 6 + u], ACT.Copy).then_inc(s_xT, 1)
                        for u in range(2):
                            gelu(JOBS + e + u, u, lambda c: b1_s[:, e + u, c:c + 1])

            @block.vector
            def _(dve):
                def finish(j, u, v, x1, bias):
                    dve.wait_ge(s_yy, j + 3)
                    dve.tensor_tensor(res[:, v], x1, psum[:, 4 + u].rearrange("p (t d) -> p t d", t=CH), ALU.add).then_inc(s_add, 1)
                    dve.wait_ge(s_add, j + 3)
                    dve.tensor_tensor(res[:, v], res[:, v], bias.unsqueeze(1).broadcast_to([P, CH, D]), ALU.add).then_inc(s_res, 1)

                def shared(b):
                    for u in range(2):
                        dve.wait_ge(s_out[u], 16 * (b + 1))
                        finish(2 * b + u, u, u, rowbuf[:, b, u * CH:(u + 1) * CH, D:2 * D], sb2_s[:])

                steps = [0]

                def own(ins):
                    ins.then_inc(s_route, 1)
                    steps[0] += 1
                    dve.wait_ge(s_route, steps[0])

                def by_token(ap):
                    return ap.rearrange("p e t -> p t e")

                def wide(ap):
                    return ap.unsqueeze(1).broadcast_to([P, E, NT])

                def choose(src, best, hot):
                    own(dve.reduce_max(best, by_token(src), AX.X))
                    own(dve.tensor_tensor(weigh[:], src, wide(best), ALU.is_equal))
                    own(dve.tensor_tensor(weigh[:], weigh[:], rank[:], ALU.mult))
                    own(dve.reduce_max(best, by_token(weigh[:]), AX.X))
                    own(dve.tensor_tensor(hot, weigh[:], wide(best), ALU.is_equal))

                def places(n, pos):
                    dve.wait_ge(s_cum, n + 1)
                    in_tile, total = psum[:, 6 + n, 0:CHOSEN], psum[:, 6 + n, CHOSEN:2 * CHOSEN]
                    own(dve.tensor_tensor_scan(incl[:].rearrange(flat), fresh[:].rearrange(flat), total, 0.0,
                                               ALU.mult, ALU.add))
                    own(dve.tensor_tensor(pos, incl[:], total.rearrange("p (e t) -> p e t", e=E), ALU.subtract))
                    own(dve.tensor_tensor(pos, pos, in_tile.rearrange("p (e t) -> p e t", e=E), ALU.add))

                def at(hot, src, dst):
                    own(dve.tensor_tensor(prod[:], hot, src, ALU.mult))
                    own(dve.reduce_sum(dst, by_token(prod[:]), AX.X))

                (best, share, place1, start1, kept, over, row1, place2, start2, taken, row2) = (small[:, i] for i in range(11))
                lg = logits[:].rearrange("p e b t -> p e (b t)")
                dve.sem_inc(s_add, 2)
                own(dve.reduce_max(best, by_token(lg), AX.X))
                own(dve.tensor_tensor(gate[:], lg, wide(best), ALU.subtract))
                dve.wait_ge(s_exp, 1)
                own(dve.reduce_sum(best, by_token(pick[:]), AX.X))
                own(dve.reciprocal(share, best))
                own(dve.tensor_tensor(gate[:], pick[:], wide(share), ALU.mult))
                choose(gate[:], best, one[:])
                dve.tensor_copy(oneb[:], one[:]).then_inc(s_one, 1)
                own(dve.scalar_tensor_tensor(out=gate[:], in0=one[:], scalar=-2.0, in1=gate[:], op0=ALU.mult, op1=ALU.add))
                choose(gate[:], best, two[:])
                places(0, pos1[:])
                at(one[:], pos1[:], place1)
                own(dve.tensor_scalar(kept, place1, float(CAP), None, ALU.is_lt))
                own(dve.tensor_scalar(over, kept, -1.0, 1.0, ALU.mult, ALU.add))
                own(dve.tensor_tensor(prod[:], two[:], wide(over), ALU.mult))
                own(dve.tensor_copy(twob[:], prod[:]))
                dve.sem_inc(s_one, 1)
                own(dve.tensor_scalar(used[:], incl[:, :, NT - 1], float(CAP), None, ALU.min))
                at(one[:], base[:], start1)
                at(two[:], base[:], start2)
                own(dve.tensor_tensor(row1, place1, start1, ALU.add))
                own(dve.tensor_tensor(row1, row1, kept, ALU.mult))
                places(1, pos2[:])
                own(dve.tensor_tensor(pos2[:], pos2[:], used[:].unsqueeze(2).broadcast_to([P, E, NT]), ALU.add))
                at(two[:], pos2[:], place2)
                own(dve.tensor_scalar(taken, place2, float(CAP), None, ALU.is_lt))
                own(dve.tensor_tensor(taken, taken, over, ALU.mult))
                own(dve.tensor_tensor(row2, place2, start2, ALU.add))
                own(dve.tensor_tensor(row2, row2, taken, ALU.mult))
                own(dve.tensor_tensor(over, over, taken, ALU.subtract))
                own(dve.tensor_tensor(over, over, own_row[:], ALU.mult))
                own(dve.tensor_tensor(row1, row1, row2, ALU.add))
                own(dve.tensor_tensor(row1, row1, over, ALU.add))
                dve.tensor_copy(slot[:], row1).then_inc(s_slot, 1)
                shared(0)
                with dve.Fori(1, B) as b:
                    shared(b)
                for u in range(2):
                    dve.wait_ge(s_out[u], 16 * (B + 1))
                with dve.Fori(0, E // BUFS) as k:
                    for v in range(BUFS):
                        dve.wait_ge(s_xs[v], 16 * (k + 1))
                        e = BUFS * k + v
                        finish(JOBS + e, v % 2, v, xs[:, v, :, D:2 * D], b2_s[:, e])


_INS = ['L0_attn_x', 'L0_attn_ln_w', 'L0_attn_ln_b', 'L0_attn_wq', 'L0_attn_wk', 'L0_attn_wv', 'L0_attn_wo',
        'L0_ffn_rw', 'L0_ffn_rb', 'L0_ffn_w1', 'L0_ffn_b1', 'L0_ffn_w2', 'L0_ffn_b2', 'L0_ffn_sw1', 'L0_ffn_sb1',
        'L0_ffn_sw2', 'L0_ffn_sb2']
_OUTS = [((4, 1024, 128), 'float32')]


def kernel(**inputs):
    import numpy as _np
    import concourse.bacc as _bacc
    from concourse import mybir as _mybir
    from concourse.bass_utils import run_bass_kernel_spmd as _run

    nc = _bacc.Bacc("TRN2", target_bir_lowering=False, num_devices=1)
    arrays, args = {}, []
    for name in _INS:
        a = _np.ascontiguousarray(inputs[name])
        arrays[f"in_{name}_dram"] = a
        args.append(nc.dram_tensor(f"in_{name}_dram", a.shape, _mybir.dt.from_np(a.dtype), kind="ExternalInput").ap())
    for i, (shape, dtype) in enumerate(_OUTS):
        dt = _mybir.dt.from_np(_np.dtype(dtype))
        args.append(nc.dram_tensor(f"out_{i}_dram", shape, dt, kind="ExternalOutput").ap())
    build(nc, *args)
    r = _run(nc, [arrays], core_ids=[0])
    got = tuple(r.results[0][f"out_{i}_dram"] for i in range(len(_OUTS)))
    return got[0]
```
